# Optimizing a Trainium2 kernel written in Bass

```python
import numpy as np
import jax
import jax.numpy as jnp

def _softmax(x, axis=-1):
    return jax.nn.softmax(x, axis=axis)

def _gelu(x):
    return jax.nn.gelu(x, approximate=True)

def _silu(x):
    return jax.nn.silu(x)

def _sigmoid(x):
    return jax.nn.sigmoid(x)

def _layernorm(x, axis=-1, eps=1e-05):
    m = jnp.mean(x, axis=axis, keepdims=True)
    v = jnp.var(x, axis=axis, keepdims=True)
    return (x - m) / jnp.sqrt(v + eps)

def _scatter_add(tgt, idx, src, axis=0):
    return tgt.at[idx].add(src)

def _segment_sum(src, seg, n):
    return jax.ops.segment_sum(src, seg, n)
kernel_name = 'mk_seq_postln_d1_jaxref_r2_db3043'

def setup_inputs(seed: int=0):
    np.random.seed(seed)
    _w = jnp.asarray

    def _L0_attn_setup():
        import jax, jax.numpy as jnp
        import numpy as np
        import math
        D_MODEL = 512
        NHEAD = 16
        M = 128
        D_K = D_MODEL // NHEAD
        EPS = 1e-06

        def create_orf(key, d_k, m):
            k1, k2 = jax.random.split(key)
            n_blocks = math.ceil(m / d_k)
            blocks = jax.random.normal(k1, (n_blocks, d_k, d_k), dtype=jnp.float32)
            q, _ = jnp.linalg.qr(blocks)
            scale = jnp.linalg.norm(jax.random.normal(k2, (m, d_k), dtype=jnp.float32), axis=1)
            return scale[:, None] * q.reshape(-1, d_k)[:m]

        def feature_map(x, orf):
            m, d_k = orf.shape
            proj = x @ orf.T / d_k ** 0.25
            norm = jnp.sum(x * x, axis=-1, keepdims=True) / (2.0 * math.sqrt(d_k))
            return (jnp.exp(proj - norm) + EPS) / math.sqrt(m)
        key = jax.random.key(seed)
        ks = jax.random.split(key, 10)
        s = 1.0 / math.sqrt(D_MODEL)
        inp = {'x': jax.random.normal(ks[0], (4, 2048, D_MODEL), dtype=jnp.float32)}
        names = ['q', 'k', 'v', 'o']
        for i, n in enumerate(names):
            inp[f'W{n}'] = jax.random.uniform(ks[1 + 2 * i], (D_MODEL, D_MODEL), dtype=jnp.float32, minval=-s, maxval=s)
            inp[f'b{n}'] = jax.random.uniform(ks[2 + 2 * i], (D_MODEL,), dtype=jnp.float32, minval=-s, maxval=s)
        inp['orf'] = create_orf(ks[9], D_K, M)
        return inp
    _L0_attn_in = _L0_attn_setup()

    def _L0_ffn_setup():
        import jax, jax.numpy as jnp
        import numpy as np
        EPS = 1e-05

        @jax.custom_vjp
        def ste_quantize(w):
            scale = jnp.maximum(jnp.mean(jnp.abs(w)), EPS)
            return jnp.clip(jnp.round(w / scale), -1.0, 1.0)

        def _ste_fwd(w):
            return (ste_quantize(w), None)

        def _ste_bwd(_, g):
            return (g,)
        ste_quantize.defvjp(_ste_fwd, _ste_bwd)
        key = jax.random.key(seed)
        k1, k2 = jax.random.split(key)
        x = jax.random.normal(k1, (8, 4096, 512), dtype=jnp.float32)
        weight = jax.random.normal(k2, (512, 512), dtype=jnp.float32) * 0.02
        return {'x': x, 'weight': weight}
    _L0_ffn_in = _L0_ffn_setup()
    _d = {'L0_attn_x': _L0_attn_in['x'], 'L0_attn_Wq': _L0_attn_in['Wq'], 'L0_attn_bq': _L0_attn_in['bq'], 'L0_attn_Wk': _L0_attn_in['Wk'], 'L0_attn_bk': _L0_attn_in['bk'], 'L0_attn_Wv': _L0_attn_in['Wv'], 'L0_attn_bv': _L0_attn_in['bv'], 'L0_attn_Wo': _L0_attn_in['Wo'], 'L0_attn_bo': _L0_attn_in['bo'], 'L0_attn_orf': _L0_attn_in['orf'], 'L0_ffn_weight': _L0_ffn_in['weight']}
    _x0 = _d['L0_attn_x']
    _d['L0_attn_x'] = jax.random.normal(jax.random.fold_in(jax.random.key(seed), 1), (8, 1024, 512), dtype=_x0.dtype)
    del _x0
    return _d

def reference(L0_attn_x, L0_attn_Wq, L0_attn_bq, L0_attn_Wk, L0_attn_bk, L0_attn_Wv, L0_attn_bv, L0_attn_Wo, L0_attn_bo, L0_attn_orf, L0_ffn_weight):

    def _L0_attn_ref(x, Wq, bq, Wk, bk, Wv, bv, Wo, bo, orf):
        import jax, jax.numpy as jnp
        import numpy as np
        import math
        D_MODEL = 512
        NHEAD = 16
        M = 128
        D_K = D_MODEL // NHEAD
        EPS = 1e-06

        def create_orf(key, d_k, m):
            k1, k2 = jax.random.split(key)
            n_blocks = math.ceil(m / d_k)
            blocks = jax.random.normal(k1, (n_blocks, d_k, d_k), dtype=jnp.float32)
            q, _ = jnp.linalg.qr(blocks)
            scale = jnp.linalg.norm(jax.random.normal(k2, (m, d_k), dtype=jnp.float32), axis=1)
            return scale[:, None] * q.reshape(-1, d_k)[:m]

        def feature_map(x, orf):
            m, d_k = orf.shape
            proj = x @ orf.T / d_k ** 0.25
            norm = jnp.sum(x * x, axis=-1, keepdims=True) / (2.0 * math.sqrt(d_k))
            return (jnp.exp(proj - norm) + EPS) / math.sqrt(m)
        B, L, D = x.shape
        H, dh = (NHEAD, D // NHEAD)

        def split(y):
            return y.reshape(B, L, H, dh).transpose(0, 2, 1, 3).reshape(B * H, L, dh)
        q = feature_map(split(x @ Wq.T + bq), orf)
        k = feature_map(split(x @ Wk.T + bk), orf)
        v = split(x @ Wv.T + bv)
        kv = jnp.einsum('nlm,nld->nmd', k, v)
        ksum = jnp.sum(k, axis=1)
        buf = jnp.concatenate([kv, ksum[..., None]], axis=-1)
        out = jnp.einsum('nlm,nmd->nld', q, buf)
        out = out[..., :-1] / out[..., -1:]
        out = out.reshape(B, H, L, dh).transpose(0, 2, 1, 3).reshape(B, L, D)
        return out @ Wo.T + bo

    def _L0_ffn_ref(x, weight):
        import jax, jax.numpy as jnp
        import numpy as np
        EPS = 1e-05

        @jax.custom_vjp
        def ste_quantize(w):
            scale = jnp.maximum(jnp.mean(jnp.abs(w)), EPS)
            return jnp.clip(jnp.round(w / scale), -1.0, 1.0)

        def _ste_fwd(w):
            return (ste_quantize(w), None)

        def _ste_bwd(_, g):
            return (g,)
        ste_quantize.defvjp(_ste_fwd, _ste_bwd)
        w_ternary = ste_quantize(weight)
        scale = jnp.maximum(jnp.mean(jnp.abs(weight)), EPS)
        return jnp.einsum('bsi,oi->bso', x, w_ternary * scale)
    x = L0_attn_x
    x = _layernorm(x + _L0_attn_ref(x, L0_attn_Wq, L0_attn_bq, L0_attn_Wk, L0_attn_bk, L0_attn_Wv, L0_attn_bv, L0_attn_Wo, L0_attn_bo, L0_attn_orf), axis=-1)
    x = _layernorm(x + _L0_ffn_ref(x, L0_ffn_weight), axis=-1)
    return x

_drawn_inputs = setup_inputs


def setup_inputs(seed=0):
    import zlib

    import numpy as np

    out = dict(_drawn_inputs(seed))
    spreads = {}
    factors = {}
    for name, (base, spread) in spreads.items():
        noise = np.random.default_rng([zlib.crc32(name.encode()), seed]).standard_normal(out[name].shape)
        drawn = base * np.exp(spread * noise) if base else spread * noise
        out[name] = jnp.asarray(drawn.astype(out[name].dtype))
    for name, factor in factors.items():
        out[name] = (out[name] * factor).astype(out[name].dtype)
    return out
```

```python
import math
from contextlib import ExitStack

import concourse.bass as bass
from concourse import mybir

F32, F32R = mybir.dt.float32, mybir.dt.float32r
ACT, ALU = mybir.ActivationFunctionType, mybir.AluOpType

B, L, D, H, DH, M = 8, 1024, 512, 16, 32, 128
P = 128
KT = D // P
TT = L // P
HG = 4
NG = H // HG
NU = 2 * NG
HALF = L // 2
EPS, LN_EPS, W_EPS = 1e-6, 1e-5, 1e-5
C_EXP = DH ** -0.25
A_SQ = math.sqrt(1.0 / (2.0 * math.sqrt(DH)) / C_EXP)
NR = 2 * HG
QK = 3 * DH + NR
KK = 2 * DH + NR


def unit_order():
    seq = [("V", t) for t in range(4)] + [("P", 1, 0), ("P", 1, 1), ("V", 4), ("N", 1)]
    seq += [("V", t) for t in range(5, TT)]
    for u in range(NU):
        if u > 0 and u + 1 < NU:
            seq.append(("P", u + 1, 0))
        if u > 0:
            seq.append(("G", u - 1, 7))
        if u > 0 and u + 1 < NU:
            seq.append(("P", u + 1, 1))
        for r in range(8):
            seq.append(("F", u, r))
            if r:
                seq.append(("G", u, r - 1))
            if r == 1 and u > 0 and u + 1 < NU:
                seq.append(("N", u + 1))
            if r == 3 and 0 < u <= NG:
                seq.append(("KVT", u - 1))
    seq.append(("G", NU - 1, 7))
    return seq


def output_order(more):
    seq = []
    for t in range(TT):
        seq.append(("O", t))
        if t >= 2:
            seq.append(("FF", t - 2))
        if t >= 1:
            seq.append(("YT", t - 1))
        if more:
            seq.append(("XT", t))
    seq.append(("FF", TT - 2))
    seq += [("P", 0, 0), ("P", 0, 1)] if more else []
    seq.append(("YT", TT - 1))
    seq += [("N", 0)] if more else []
    seq.append(("FF", TT - 1))
    return seq


PROLOGUE = [("XT", t) for t in range(TT)] + [("P", 0, 0), ("P", 0, 1), ("N", 0)]
BODY = unit_order() + output_order(True)
LAST = unit_order() + output_order(False)

RING = {"V": "pj", "P": "pj", "O": "pj", "FF": "pj", "F": "ft", "XT": "ft", "YT": "ft", "N": "nb", "KVT": "nb"}
RING_SIZE = {"pj": 2, "ft": 2, "nb": 1}


def bank_uses(seq, before):
    uses = {ring: list(before[ring]) for ring in RING_SIZE}
    out = []
    for n, stage in enumerate(seq):
        ring = RING.get(stage[0])
        if ring is None:
            out.append((None, None))
            continue
        size = RING_SIZE[ring]
        mine = uses[ring]
        old = mine[-size] if len(mine) >= size else None
        out.append(((len(mine) - len(before[ring])) % size, old))
        mine.append((n, stage))
    return out


def tail(seq):
    out = {}
    for ring, size in RING_SIZE.items():
        mine = [(None, s) for s in seq if RING.get(s[0]) == ring]
        out[ring] = mine[-size:]
    return out


def attention_kernel(nc, x, Wq, bq, Wk, bk, Wv, bv, Wo, bo, orf, wff, out):
    x_tiles = x.rearrange("b (t p) d -> b t p d", p=P)
    out_tiles = out.rearrange("b (t p) d -> b t p d", p=P)

    ctx = ExitStack()
    with ctx:
        def sb(name, shape, dt=F32):
            return ctx.enter_context(nc.sbuf_tensor(name, shape, dt))

        def sem(name):
            return ctx.enter_context(nc.semaphore(name))

        WH = {w: sb(f"W{w}_hi", [P, KT, D], F32R) for w in "qkvo"}
        WL = {w: sb(f"W{w}_lo", [P, KT, D], F32R) for w in "qkvo"}
        WT3 = sb("W_ternary", [P, KT, D], F32R)
        XH, XL = sb("x_hi", [P, KT, L], F32R), sb("x_lo", [P, KT, L], F32R)
        VA = sb("values_then_attention", [P, TT, D])
        ST = sb("stacks", [P, 2, 4 * L], F32R)
        EH, EL = sb("unit_hi", [P, L], F32R), sb("unit_lo", [P, L], F32R)
        SQ = sb("squares_then_x", [P, L])
        FE = sb("features", [P, 4, HG, M + 1])
        XR = sb("rows", [P, 4, D])
        BO = sb("out_bias", [P, D])
        ident = sb("ident", [P, P])
        WQS = sb("orf_query", [P, HG, M], F32R)
        MA = sb("orf_key_a", [P, 2 * M], F32R)
        MB = sb("orf_key_b", [P, 2, 2 * M], F32R)
        NP_ = sb("norm_columns", [P, DH])
        ones = sb("ones", [P, P])
        KVS = sb("kv_ksum", [P, NG, 2 * P])
        KVT = sb("kv_ksum_t", [P, 2 * P])
        NH, NN = sb("norm_hi", [P, 2 * P], F32R), sb("norm_rows", [P, 2 * P], F32R)
        DR = sb("den", [P, 2, HALF])
        cols = sb("cols", [P, 128])

        def col(a, n=1):
            return cols[:, a:a + n]

        BC, ABC, BVC = col(0, NU), col(NU, NU), col(2 * NU, KT)
        NEGM, EPSL, EXPO, EV = col(20), col(21), col(22), col(23)
        WSUM, SC, HS, NHS = col(24), col(25), col(26), col(27)
        RSUM, CC = col(28, 2 * NG), col(36, 2 * NG)
        stats = sb("stats", [P, 2, 4, 12])

        def ln(kind, t, a, n=1):
            return stats[:, kind, t % 4, a:a + n]

        PS = [ctx.enter_context(nc.psum_tensor(f"ps{i}", [P, 512], F32)) for i in range(8)]
        BANKS = {"pj": PS[0:2], "ft": PS[2:4], "nb": PS[4:5]}
        ND, DN = PS[5:7], PS[7]

        class Signal:

            def __init__(self, name, per, credit=0, step=1):
                self.sem, self.per, self.credit, self.step = sem(name), per, credit, step

            def nth(self, batch, k):
                return batch[0] * (self.per * self.step) + (self.credit + k + batch[1] * self.per) * self.step

        t_xt, t_v, t_p = Signal("xt_done", TT), Signal("v_done", TT), Signal("p_done", 2 * NU)
        t_n, t_kvt = Signal("n_done", NU, 1), Signal("kvt_done", NG, 1)
        t_f, t_g = Signal("f_done", 8 * NU, 9), Signal("g_done", 8 * NU, 4)
        t_o, t_yt, t_ff = Signal("o_done", TT), Signal("yt_done", TT), Signal("ff_done", TT, 1)
        a_xhi, a_v, a_p = Signal("x_hi_ready", TT), Signal("v_ready", TT), Signal("unit_hi_sq_ready", 4 * NU)
        a_exp, a_kc = Signal("features_ready", 8 * NU), Signal("kv_copied", 3 * NG)
        a_den, a_ahi = Signal("den_copied", 2 * NG, 1), Signal("a_hi_ready", TT)
        a_y, a_yhi, a_out = Signal("y_ready", TT), Signal("y_hi_ready", TT), Signal("out_ready", TT)
        v_xlo, v_plo, v_n = Signal("x_lo_ready", TT), Signal("unit_lo_ready", 2 * NU), Signal("norms_ready", 2 * NU)
        v_kvc, v_c = Signal("kv_ready", NG), Signal("eps_sums_ready", NG)
        v_rc, v_a = Signal("reciprocal_ready", 2 * NG), Signal("attention_ready", 2 * NG, 2)
        v_alo, v_ylo = Signal("a_lo_ready", TT, TT), Signal("y_lo_ready", TT, 1)
        v_ln = [Signal("ln1_steps", 5 * TT), Signal("ln2_steps", 5 * TT, 4)]
        g_xb = Signal("x_plus_bias_ready", TT)
        g_ln = [Signal("ln1_scale_ready", 2 * TT), Signal("ln2_scale_ready", 2 * TT)]
        d_xl = [Signal(f"x_loaded{s}", TT // 2, 0, 16) for s in range(2)]
        d_xr = [Signal(f"rows_loaded{s}", TT // 4, 0, 16) for s in range(4)]
        d_st = [Signal(f"rows_stored{s}", TT // 4, 1, 16) for s in range(4)]
        KEY_LIFTS, QUERY_LIFTS = 10, 12
        lifted = [Signal(f"stack_lifted{s}", 2 * (KEY_LIFTS + QUERY_LIFTS), 1, 16) for s in range(2)]
        n_lifted = [Signal(f"norms_lifted{s}", 4 * NG, 1, 16) for s in range(2)]

        def lifts(u):
            n = u // 2 + 1
            return KEY_LIFTS * min(n, 2) + QUERY_LIFTS * max(n - 2, 0)

        def unit_lifted(eng, j, u):
            if u < 0:
                eng.wait_ge(lifted[1].sem, lifted[1].nth(j, 0))
            else:
                eng.wait_ge(lifted[u % 2].sem, lifted[u % 2].nth(j, lifts(u)))

        def norms_lifted(eng, j, u):
            if u < 0:
                eng.wait_ge(n_lifted[1].sem, n_lifted[1].nth(j, 0))
            else:
                eng.wait_ge(n_lifted[u % 2].sem, n_lifted[u % 2].nth(j, 4 * (u // 2 + 1)))

        s_ld, s_k, s_pe, s_act, s_dve, s_pool = (sem(n) for n in (
            "setup_loaded", "setup_consts", "setup_pe", "setup_act", "setup_dve", "setup_pool"))
        s_wlo, s_chain, s_bv = sem("setup_w_lo"), sem("setup_chain"), sem("setup_bv")
        s_go, s_pin = sem("setup_finished"), sem("carries_a_wait")
        s_ld2 = [sem(f"setup_w{n}") for n in range(5)]

        WS = [VA[:, 4 * n:4 * n + 4, :] for n in range(2)]
        sources = [Wq, Wk, Wv, Wo, wff]
        orf_rep = DR[:, 1, 0:P]
        bv_rep = DR[:, 0, :]
        lo_rows = FE[:, 1, 0, 0:4 * HG]

        def old_bank(stage, j):
            kind, k = stage[0], stage[1]
            if kind == "V":
                return a_v, a_v.nth(j, k + 1)
            if kind == "P":
                return v_plo, v_plo.nth(j, 2 * k + stage[2] + 1)
            if kind == "O":
                return v_ln[0], v_ln[0].nth(j, 5 * k + 1)
            if kind == "FF":
                return v_ln[1], v_ln[1].nth(j, 5 * k + 1)
            if kind == "F":
                return a_exp, a_exp.nth(j, 8 * k + stage[2] + 1)
            if kind == "XT":
                return v_xlo, v_xlo.nth(j, k + 1)
            if kind == "YT":
                return v_ylo, v_ylo.nth(j, k + 1)
            if kind == "N":
                return v_n, v_n.nth(j, 2 * k + 2)
            return v_kvc, v_kvc.nth(j, k + 1)

        def looks_ahead(stage):
            return stage[0] == "XT" or stage[:2] in (("P", 0), ("N", 0))

        none = {ring: [] for ring in RING_SIZE}
        BANKING = {id(PROLOGUE): bank_uses(PROLOGUE, none), id(BODY): bank_uses(BODY, tail(BODY)),
                   id(LAST): bank_uses(LAST, tail(BODY))}

        def steps(seq, j):
            for n, (stage, (bank, old)) in enumerate(zip(seq, BANKING[id(seq)])):
                mine = (j, 1) if seq is BODY and looks_ahead(stage) else (j, 0)
                if old is not None:
                    m, prev = old
                    if m is None:
                        old = (prev, (j, 0 if looks_ahead(prev) else -1))
                    else:
                        old = (prev, (j, 1 if seq is BODY and looks_ahead(prev) else 0))
                yield stage, mine, (None if bank is None else BANKS[RING[stage[0]]][bank]), old

        def batches(eng, program):
            program(PROLOGUE, 0)
            with eng.Fori(0, B - 1) as i:
                program(BODY, i)
            program(LAST, B - 1)

        block = ctx.enter_context(nc.Block())

        @block.sync
        def _(sp):
            sp.dma_start(BC[:, 0:NG], bk.rearrange("(g p) -> p g", p=P), allow_slow_non_contiguous=True).then_inc(s_ld, 16)
            sp.dma_start(BC[:, NG:NU], bq.rearrange("(g p) -> p g", p=P), allow_slow_non_contiguous=True).then_inc(s_ld, 16)
            sp.dma_start(BVC, bv.rearrange("(g p) -> p g", p=P), allow_slow_non_contiguous=True).then_inc(s_ld, 16)
            sp.dma_start(BO[:, :], bo.unsqueeze(0).broadcast_to([P, D])).then_inc(s_ld, 16)
            for r in range(4):
                sp.dma_start(orf_rep[:, DH * r:DH * (r + 1)], orf).then_inc(s_ld, 16)
            for n, w in enumerate(sources):
                if n >= 2:
                    sp.wait_ge(s_pe, 4 * (n - 1) + 1)
                sp.dma_start(WS[n % 2], w.rearrange("(a p) i -> p a i", p=P)).then_inc(s_ld2[n], 16)
            for sig in lifted + n_lifted:
                sp.sem_inc(sig.sem, sig.credit * sig.step)

            def wait(semaphore, value):
                sp.wait_ge(semaphore, value)
                sp.sem_inc(s_pin, 1)

            def load_x(j, t):
                sig = d_xl[t % 2]
                sp.dma_start(SQ[:, 512 * (t % 2):512 * (t % 2 + 1)], x_tiles[j[0] + j[1], t]).then_inc(sig.sem, 16)

            def load_rows(j, t):
                wait(d_st[t % 4].sem, d_st[t % 4].nth(j, t // 4))
                sp.dma_start(XR[:, t % 4, :], x_tiles[j[0] + j[1], t]).then_inc(d_xr[t % 4].sem, 16)

            def program(seq, i):
                if seq is PROLOGUE:
                    load_x((0, 0), 0)
                    load_x((0, 0), 1)
                for stage, j, _, _ in steps(seq, i):
                    kind, u = stage[0], stage[1]
                    if kind == "XT" and u + 2 < TT:
                        wait(t_xt.sem, t_xt.nth(j, u + 1))
                        load_x(j, u + 2)
                    elif kind == "FF" and u + 4 < TT:
                        load_rows(j, u + 4)
                    elif kind == "P" and stage[2] == 1:
                        slot = ST[:, u % 2, :].bitcast(F32)
                        hi, lo, sig = EH[:, :].bitcast(F32), EL[:, :].bitcast(F32), lifted[u % 2]
                        wait(t_f.sem, t_f.nth(j, 8 * (u - 1)))
                        if u == 1:
                            wait(t_ff.sem, t_ff.nth(j, 0))
                        wait(a_p.sem, a_p.nth(j, 4 * u + 3))
                        for h in range(HG):
                            src = hi[DH * h:DH * (h + 1), :]
                            if u < NG:
                                r, c = 2 * DH * (h % 2), L * (h // 2)
                                sp.dma_start(slot[r:r + DH, c:c + L], src).then_inc(sig.sem, 16)
                            else:
                                sp.dma_start(slot[0:DH, L * h:L * (h + 1)], src).then_inc(sig.sem, 16)
                                sp.dma_start(slot[2 * DH:3 * DH, L * h:L * (h + 1)], src).then_inc(sig.sem, 16)
                        if u < NG:
                            for p in range(2):
                                sp.dma_start(slot[0:2 * DH, L * (2 + p):L * (3 + p)],
                                             hi[2 * DH * p:2 * DH * (p + 1), :]).then_inc(sig.sem, 16)
                        wait(v_plo.sem, v_plo.nth(j, 2 * u + 2))
                        for h in range(HG):
                            r, c = (2 * DH * (h % 2) + DH, L * (h // 2)) if u < NG else (DH, L * h)
                            sp.dma_start(slot[r:r + DH, c:c + L], lo[DH * h:DH * (h + 1), :]).then_inc(sig.sem, 16)
                    elif kind == "N":
                        slot = ST[:, u % 2, :].bitcast(F32)
                        wait(v_n.sem, v_n.nth(j, 2 * u + 2))
                        for c in range(4):
                            src = NN[DH * c:DH * c + NR, :].bitcast(F32).unsqueeze(1)
                            if u < NG:
                                dst = slot[2 * DH:2 * DH + NR, 2 * L:4 * L].rearrange("p (a t) -> p a t", a=2)
                                n = 2
                            else:
                                dst = slot[3 * DH:3 * DH + NR, :].rearrange("p (a t) -> p a t", a=HG)
                                n = HG
                            sp.dma_start(dst[:, :, 256 * c:256 * (c + 1)],
                                         src.broadcast_to([NR, n, 256])).then_inc(n_lifted[u % 2].sem, 16)
                        if u == NU - 1:
                            for t in range(4):
                                load_rows(j, t)
                            if seq is BODY:
                                wait(t_n.sem, t_n.nth(j, NU))
                                load_x((i, 1), 0)
                                load_x((i, 1), 1)

            batches(sp, program)

        @block.gpsimd
        def _(pool):
            filled = [1]

            def fill_where(t, base, pattern, cm, fill):
                pool.wait_ge(s_k, filled[0])
                filled[0] += 1
                nc.gpsimd.affine_select(out=t, in_=t, compare_op=ALU.not_equal, fill=fill, base=base,
                                        pattern=pattern, channel_multiplier=cm).then_inc(s_k, 1)

            nc.gpsimd.memset(ident[:, :], 0.0)
            nc.gpsimd.memset(ones[:, :], 1.0)
            nc.gpsimd.memset(NP_[:, :], 0.0)
            nc.gpsimd.memset(lo_rows, 0.0)
            nc.gpsimd.memset(FE[:, 2, :, :], 0.0)
            nc.gpsimd.memset(EXPO, -0.5)
            nc.gpsimd.memset(EPSL, EPS * L)
            for t in (WQS, MA, MB):
                last = nc.gpsimd.memset(t[:].bitcast(F32), 0.0)
            last.then_inc(s_k, 1)
            fill_where(ident[:, :], 0, [[-1, P]], 1, 1.0)
            pool.wait_ge(s_k, filled[0])
            filled[0] += 1
            for h in range(HG):
                nc.gpsimd.memset(NP_[DH * h:DH * (h + 1), h:h + 1], 1.0)
                last = nc.gpsimd.memset(NP_[DH * h:DH * (h + 1), HG + h:HG + h + 1], 1.0)
            last.then_inc(s_k, 1)
            fill_where(lo_rows.rearrange("p (a b) -> p a b", a=4), -HG, [[-DH, 4], [-1, HG]], 1, -1.0)
            q_rows = FE[3 * DH:QK, 2, :, 0:M]
            fill_where(q_rows, 0, [[-1, HG], [0, M]], 1, -1.0)
            fill_where(q_rows, -HG, [[-1, HG], [0, M]], 1, -1.0)
            k_rows = FE[2 * DH:KK, 2, :, 0:M]
            fill_where(k_rows, 0, [[-1, HG], [0, M]], 1, -1.0)
            fill_where(k_rows, -HG, [[-1, HG], [0, M]], 1, -1.0)
            pool.wait_ge(s_k, filled[0])
            pool.wait_ge(s_dve, 1)
            pool.wait_ge(s_pe, 1)
            nc.gpsimd.memset(FE[:, :, :, M:M + 1], 1.0).then_inc(s_pool, 1)

            def layer_scale(k, j, t):
                pool.wait_ge(v_ln[k].sem, v_ln[k].nth(j, 5 * t + 5))
                nc.gpsimd.tensor_tensor(ln(k, t, 10), ln(k, t, 8), EXPO, ALU.pow).then_inc(g_ln[k].sem, 1)
                pool.wait_ge(g_ln[k].sem, g_ln[k].nth(j, 2 * t + 1))
                nc.gpsimd.tensor_tensor(ln(k, t, 11), ln(k, t, 9), ln(k, t, 10), ALU.mult).then_inc(g_ln[k].sem, 1)

            def program(seq, i):
                for stage, j, _, _ in steps(seq, i):
                    kind, t = stage[0], stage[1]
                    if kind == "O":
                        pool.wait_ge(d_xr[t % 4].sem, d_xr[t % 4].nth(j, t // 4 + 1))
                        nc.gpsimd.tensor_tensor(XR[:, t % 4, :], XR[:, t % 4, :], BO[:, :], ALU.add).then_inc(g_xb.sem, 1)
                        layer_scale(0, j, t)
                    elif kind == "FF":
                        layer_scale(1, j, t)

            pool.wait_ge(s_dve, 4)
            batches(pool, program)

        @block.scalar
        def _(act):
            for sig in (a_den,):
                act.sem_inc(sig.sem, sig.credit)
            for sig in d_st:
                act.sem_inc(sig.sem, sig.credit * sig.step)
            for n in range(4):
                w = "qkvo"[n]
                for k in range(KT):
                    act.wait_ge(s_pe, 4 * n + k + 2)
                    nc.scalar.activation(WH[w][:, k, :], PS[(4 * n + k) % 4][:, :], ACT.Copy).then_inc(s_act, 1)
            act.wait_ge(s_ld2[4], 16)
            nc.scalar.activation(XR[:, :, :].rearrange("p a i -> p (a i)"), WS[0].rearrange("p a i -> p (a i)"), ACT.Abs,
                                 accum_out=WSUM).then_inc(s_act, 1)
            act.wait_ge(s_go, 1)

            def program(seq, i):
                for stage, j, ps, _ in steps(seq, i):
                    kind, u = stage[0], stage[1]
                    if kind == "XT":
                        act.wait_ge(t_xt.sem, t_xt.nth(j, u + 1))
                        nc.scalar.activation(XH[:, :, P * u:P * (u + 1)], ps[:, :].rearrange("p (k c) -> p k c", k=KT),
                                             ACT.Copy).then_inc(a_xhi.sem, 1)
                    elif kind == "V":
                        act.wait_ge(t_v.sem, t_v.nth(j, u + 1))
                        act.wait_ge(v_alo.sem, v_alo.nth(j, u + 1 - TT))
                        nc.scalar.activation(VA[:, u, :], ps[:, :], ACT.Copy).then_inc(a_v.sem, 1)
                    elif kind == "P":
                        h, half = stage[2], slice(HALF * stage[2], HALF * (stage[2] + 1))
                        act.wait_ge(t_p.sem, t_p.nth(j, 2 * u + h + 1))
                        if h == 0:
                            unit_lifted(act, j, u - 1)
                        nc.scalar.activation(EH[:, half], ps[:, :], ACT.Identity, bias=BC[:, u:u + 1]).then_inc(a_p.sem, 1)
                        if h == 0:
                            act.wait_ge(t_n.sem, t_n.nth(j, u))
                        nc.scalar.activation(SQ[:, half], ps[:, :], ACT.Square, bias=ABC[:, u:u + 1],
                                             scale=A_SQ).then_inc(a_p.sem, 1)
                    elif kind == "F":
                        n = 8 * u + stage[2]
                        act.wait_ge(t_f.sem, t_f.nth(j, n + 1))
                        act.wait_ge(t_g.sem, t_g.nth(j, n + 1 - 4))
                        nc.scalar.activation(FE[:, n % 4, :, 0:M], ps[:, :].rearrange("p (a m) -> p a m", a=HG),
                                             ACT.Exp, scale=C_EXP).then_inc(a_exp.sem, 1)
                    elif kind == "G" and u < NG and stage[2] == 7:
                        kv = ND[u % 2]
                        act.wait_ge(t_g.sem, t_g.nth(j, 8 * u + 8))
                        nc.scalar.activation(EV, kv[:, M:M + 1], ACT.Copy, scale=EPS).then_inc(a_kc.sem, 1)
                        act.wait_ge(t_kvt.sem, t_kvt.nth(j, u))
                        act.wait_ge(a_kc.sem, a_kc.nth(j, 3 * u + 1))
                        nc.scalar.activation(KVT[:, 0:M], kv[:, 0:M], ACT.Identity, bias=EV,
                                             accum_out=RSUM[:, 2 * u:2 * u + 1]).then_inc(a_kc.sem, 1)
                        nc.scalar.activation(KVT[:, M:2 * M], kv[:, 2 * M:3 * M], ACT.Identity, bias=EPSL,
                                             accum_out=RSUM[:, 2 * u + 1:2 * u + 2]).then_inc(a_kc.sem, 1)
                    elif kind == "G" and u >= NG and stage[2] % 4 == 3:
                        g, h = u - NG, stage[2] // 4
                        act.wait_ge(t_g.sem, t_g.nth(j, 8 * u + stage[2] + 1))
                        if h == 0:
                            act.wait_ge(v_c.sem, v_c.nth(j, g + 1))
                        act.wait_ge(v_a.sem, v_a.nth(j, 2 * g + h - 1))
                        nc.scalar.activation(DR[:, h, :], DN[:, :], ACT.Identity,
                                             bias=CC[:, 2 * g + 1:2 * g + 2]).then_inc(a_den.sem, 1)
                    elif kind == "O":
                        for t in ([0, 1] if u == 0 else [u + 1]):
                            if t < TT:
                                split_hi(j, t)
                        if u >= 1:
                            apply_norm(0, j, u - 1)
                    elif kind == "YT":
                        act.wait_ge(t_yt.sem, t_yt.nth(j, u + 1))
                        nc.scalar.activation(ST[:, 1, 2048:2560], ps[:, :], ACT.Copy).then_inc(a_yhi.sem, 1)
                        if u >= 2:
                            store_rows(j, u - 2)
                    elif kind == "FF" and u == TT - 2:
                        apply_norm(0, j, u + 1)
                    elif kind == "FF" and u == TT - 1:
                        store_rows(j, u - 1)
                        store_rows(j, u)

            def split_hi(j, t):
                act.wait_ge(v_a.sem, v_a.nth(j, 7 if t < 4 else 8))
                if t < 2:
                    act.wait_ge(t_f.sem, t_f.nth(j, 8 * NU))
                else:
                    act.wait_ge(t_o.sem, t_o.nth(j, t - 1))
                nc.scalar.activation(ST[:, 1, D * (t % 2):D * (t % 2 + 1)], VA[:, t, :], ACT.Copy).then_inc(a_ahi.sem, 1)

            def apply_norm(k, j, t):
                act.wait_ge(g_ln[k].sem, g_ln[k].nth(j, 2 * t + 2))
                row = XR[:, t % 4, :]
                nc.scalar.activation(row, row, ACT.Identity, scale=ln(k, t, 10), bias=ln(k, t, 11))\
                    .then_inc((a_y, a_out)[k].sem, 1)

            def store_rows(j, t):
                apply_norm(1, j, t)
                act.wait_ge(a_out.sem, a_out.nth(j, t + 1))
                act.dma_start(out_tiles[j[0] + j[1], t], XR[:, t % 4, :]).then_inc(d_st[t % 4].sem, 16)

            batches(act, program)
            for sig in d_st:
                act.wait_ge(sig.sem, sig.nth((B, 0), 0))

        @block.vector
        def _(dve):
            for sig in (v_a, v_alo, v_ylo, v_ln[1]):
                dve.sem_inc(sig.sem, sig.credit)
            chain = [0]

            def link(ins):
                chain[0] += 1
                ins.then_inc(s_chain, 1)
                dve.wait_ge(s_chain, chain[0])

            dve.wait_ge(s_k, 8)
            nc.vector.reduce_sum(NEGM, lo_rows, axis=mybir.AxisListType.X)
            dve.wait_ge(s_ld, 16 * 8)
            nc.vector.tensor_scalar(ABC, BC, A_SQ, None, ALU.mult)
            for k in range(KT):
                last = nc.vector.tensor_scalar(bv_rep[:, P * k:P * (k + 1)], ones[:, :], BVC[:, k:k + 1], None, ALU.mult)
            last.then_inc(s_bv, 1)
            dve.wait_ge(s_pe, 1)
            wT = PS[7]
            for r in range(2):
                for h in range(HG):
                    nc.vector.tensor_copy(WQS[DH * r:DH * (r + 1), h, :], wT[DH * r:DH * (r + 1), 0:M])
            for r in range(4):
                a = r // 2
                nc.vector.tensor_copy(MA[DH * r:DH * (r + 1), M * a:M * (a + 1)], wT[DH * r:DH * (r + 1), 0:M])
            link(nc.vector.tensor_copy(EH[:, 0:M], wT[:, 0:M]))
            for h in range(HG):
                r = slice(2 * DH, 3 * DH)
                nc.vector.tensor_tensor(WQS[r, h, :], wT[r, 0:M], EH[r, 0:M].bitcast(F32), ALU.subtract)
            for p in range(2):
                for a in range(2):
                    r = slice(DH * a, DH * (a + 1))
                    nc.vector.tensor_tensor(MB[r, p, M * a:M * (a + 1)], wT[r, 0:M], EH[r, 0:M].bitcast(F32), ALU.subtract)
            nc.vector.tensor_copy(WQS[3 * DH:QK, :, :], FE[3 * DH:QK, 2, :, 0:M])
            last = nc.vector.tensor_copy(MB[2 * DH:KK, :, :].rearrange("p a (b m) -> p (a b) m", b=2),
                                         FE[2 * DH:KK, 2, :, 0:M])
            last.then_inc(s_dve, 1)
            for n in range(4):
                w = "qkvo"[n]
                for k in range(KT):
                    dve.wait_ge(s_act, 4 * n + k + 1)
                    nc.vector.tensor_tensor(WL[w][:, k, :], PS[(4 * n + k) % 4][:, :], WH[w][:, k, :].bitcast(F32),
                                            ALU.subtract).then_inc(s_wlo, 1)
            dve.wait_ge(s_pe, 4 * 4 + 2)
            link(nc.vector.tensor_scalar(SC, PS[6][:, 0:1], 1.0 / (D * D), W_EPS, ALU.mult, ALU.max))
            link(nc.vector.tensor_scalar(HS, SC, 0.5, None, ALU.mult))
            link(nc.vector.tensor_scalar(NHS, SC, -0.5, None, ALU.mult))
            wf = WS[0].rearrange("p a i -> p (a i)")
            below = WS[1].rearrange("p a i -> p (a i)")
            link(nc.vector.tensor_scalar(below, wf, NHS, None, ALU.is_lt))
            nc.vector.scalar_tensor_tensor(out=wf, in0=wf, scalar=HS, in1=below, op0=ALU.is_gt,
                                           op1=ALU.subtract).then_inc(s_dve, 1)
            for k in range(KT):
                dve.wait_ge(s_pe, 4 * 4 + 3 + k)
                last = nc.vector.tensor_copy(WT3[:, k, :], PS[k][:, :])
            last.then_inc(s_dve, 1)
            dve.wait_ge(s_pe, 4 * 4 + 3 + KT)
            nc.vector.tensor_tensor(BO[:, :], PS[7][:, :], BO[:, :], ALU.add).then_inc(s_dve, 1)
            dve.wait_ge(s_pool, 1)
            dve.wait_ge(s_dve, 4)
            dve.sem_inc(s_go, 1)

            def layer_stats(k, j, t, source):
                sig, row, n = v_ln[k], XR[:, t % 4, :], 5 * t
                source().then_inc(sig.sem, 1)
                dve.wait_ge(sig.sem, sig.nth(j, n + 1))
                nc.vector.bn_stats(ln(k, t, 0, 6), row).then_inc(sig.sem, 1)
                dve.wait_ge(sig.sem, sig.nth(j, n + 2))
                dve.sem_inc(s_pin, 1)
                nc.vector.bn_aggr(ln(k, t, 6, 2), ln(k, t, 0, 6)).then_inc(sig.sem, 1)
                dve.wait_ge(sig.sem, sig.nth(j, n + 3))
                nc.vector.tensor_scalar(ln(k, t, 8), ln(k, t, 7), LN_EPS, None, ALU.add).then_inc(sig.sem, 1)
                nc.vector.tensor_scalar(ln(k, t, 9), ln(k, t, 6), -1.0, None, ALU.mult).then_inc(sig.sem, 1)

            def split_lo(j, t):
                dve.wait_ge(a_ahi.sem, a_ahi.nth(j, t + 1))
                nc.vector.tensor_tensor(ST[:, 1, 1024 + D * (t % 2):1024 + D * (t % 2 + 1)], VA[:, t, :],
                                        ST[:, 1, D * (t % 2):D * (t % 2 + 1)].bitcast(F32), ALU.subtract).then_inc(v_alo.sem, 1)

            def program(seq, i):
                for stage, j, ps, _ in steps(seq, i):
                    kind, u = stage[0], stage[1]
                    if kind == "XT":
                        dve.wait_ge(a_xhi.sem, a_xhi.nth(j, u + 1))
                        c = slice(P * u, P * (u + 1))
                        nc.vector.tensor_tensor(XL[:, :, c], ps[:, :].rearrange("p (k c) -> p k c", k=KT),
                                                XH[:, :, c].bitcast(F32), ALU.subtract).then_inc(v_xlo.sem, 1)
                    elif kind == "P":
                        h, half = stage[2], slice(HALF * stage[2], HALF * (stage[2] + 1))
                        dve.wait_ge(a_p.sem, a_p.nth(j, 2 * (2 * u + h) + 2))
                        if h == 0:
                            unit_lifted(dve, j, u - 1)
                        nc.vector.scalar_tensor_tensor(out=EL[:, half], in0=ps[:, :], scalar=BC[:, u:u + 1],
                                                       in1=EH[:, half].bitcast(F32), op0=ALU.add,
                                                       op1=ALU.subtract).then_inc(v_plo.sem, 1)
                    elif kind == "N":
                        dve.wait_ge(t_n.sem, t_n.nth(j, u + 1))
                        norms_lifted(dve, j, u - 1)
                        nc.vector.tensor_copy(NH[:, :], ps[:, 0:256]).then_inc(v_n.sem, 1)
                        dve.wait_ge(v_n.sem, v_n.nth(j, 2 * u + 1))
                        nc.vector.scalar_tensor_tensor(out=NN[:, :], in0=NH[:, :].bitcast(F32), scalar=NEGM,
                                                       in1=ps[:, 0:256], op0=ALU.mult, op1=ALU.add).then_inc(v_n.sem, 1)
                    elif kind == "KVT":
                        dve.wait_ge(t_kvt.sem, t_kvt.nth(j, u + 1))
                        nc.vector.tensor_copy(KVS[:, u, :], ps[:, 0:256]).then_inc(v_kvc.sem, 1)
                    elif kind == "G" and u < NG and stage[2] == 7:
                        dve.wait_ge(a_kc.sem, a_kc.nth(j, 3 * u + 3))
                        nc.vector.tensor_scalar(CC[:, 2 * u:2 * u + 2], RSUM[:, 2 * u:2 * u + 2], EPS, None,
                                                ALU.mult).then_inc(v_c.sem, 1)
                    elif kind == "G" and u >= NG and stage[2] % 4 == 3:
                        g, h = u - NG, stage[2] // 4
                        dve.wait_ge(a_den.sem, a_den.nth(j, 2 * g + h + 1))
                        nc.vector.reciprocal(DR[:, h, :], DR[:, h, :]).then_inc(v_rc.sem, 1)
                        dve.wait_ge(v_rc.sem, v_rc.nth(j, 2 * g + h + 1))
                        nc.vector.scalar_tensor_tensor(
                            out=VA[:, 4 * h:4 * h + 4, P * g:P * (g + 1)], in0=ND[h][:, :].rearrange("p (t c) -> p t c", t=4),
                            scalar=CC[:, 2 * g:2 * g + 1], in1=DR[:, h, :].rearrange("p (t c) -> p t c", t=4),
                            op0=ALU.add, op1=ALU.mult).then_inc(v_a.sem, 1)
                    elif kind == "O":
                        for t in ([0, 1] if u == 0 else [u + 1]):
                            if t < TT:
                                split_lo(j, t)
                        dve.wait_ge(t_o.sem, t_o.nth(j, u + 1))
                        dve.wait_ge(g_xb.sem, g_xb.nth(j, u + 1))
                        row = XR[:, u % 4, :]
                        layer_stats(0, j, u, lambda: nc.vector.tensor_tensor(row, ps[:, :], row, ALU.add))
                    elif kind == "YT":
                        dve.wait_ge(a_yhi.sem, a_yhi.nth(j, u + 1))
                        nc.vector.tensor_tensor(ST[:, 1, 2560:3072], ps[:, :], ST[:, 1, 2048:2560].bitcast(F32),
                                                ALU.subtract).then_inc(v_ylo.sem, 1)
                    elif kind == "FF":
                        dve.wait_ge(t_ff.sem, t_ff.nth(j, u + 1))
                        row = XR[:, u % 4, :]
                        layer_stats(1, j, u, lambda: nc.vector.scalar_tensor_tensor(
                            out=row, in0=ps[:, :], scalar=SC, in1=row, op0=ALU.mult, op1=ALU.add))

            batches(dve, program)

        @block.tensor
        def _(pe):
            for sig in (t_n, t_kvt, t_f, t_g, t_ff):
                pe.sem_inc(sig.sem, sig.credit)
            mm = nc.tensor.matmul
            pe.wait_ge(s_k, 8)
            pe.wait_ge(s_ld, 16 * 8)
            nc.tensor.transpose(PS[7][:, 0:M], orf_rep, ident[:, :]).then_inc(s_pe, 1)
            for n in range(4):
                pe.wait_ge(s_ld2[n], 16)
                for k in range(KT):
                    m = 4 * n + k
                    if m >= 4:
                        pe.wait_ge(s_wlo, m - 3)
                    for a in range(KT):
                        last = nc.tensor.transpose(PS[m % 4][:, P * a:P * (a + 1)], WS[n % 2][:, a, P * k:P * (k + 1)], ident[:, :])
                    last.then_inc(s_pe, 1)
            pe.wait_ge(s_act, 17)
            mm(PS[6][:, 0:1], ones[:, :], WSUM, start=True, stop=True).then_inc(s_pe, 1)
            pe.wait_ge(s_dve, 2)
            pe.wait_ge(s_wlo, 16)
            for k in range(KT):
                for a in range(KT):
                    last = nc.tensor.transpose(PS[k][:, P * a:P * (a + 1)], WS[0][:, a, P * k:P * (k + 1)], ident[:, :])
                last.then_inc(s_pe, 1)
            pe.wait_ge(s_bv, 1)
            pe.wait_ge(s_dve, 1)
            for k in range(KT):
                for n, w in enumerate((WH["o"], WL["o"])):
                    last = mm(PS[7][:, :], bv_rep[:, P * k:P * (k + 1)], w[:, k, :].bitcast(F32), start=(k == 0 and n == 0),
                              stop=(k == KT - 1 and n == 1))
            last.then_inc(s_pe, 1)
            pe.wait_ge(s_go, 1)

            def products(out, terms):
                for n, (a, b) in enumerate(terms):
                    last = mm(out, a, b, start=(n == 0), stop=(n == len(terms) - 1))
                return last

            def program(seq, i):
                for stage, j, ps, old in steps(seq, i):
                    kind, u = stage[0], stage[1]
                    if old is not None:
                        sig, value = old_bank(*old)
                        pe.wait_ge(sig.sem, value)
                    if kind == "XT":
                        pe.wait_ge(d_xl[u % 2].sem, d_xl[u % 2].nth(j, u // 2 + 1))
                        for k in range(KT):
                            c = 512 * (u % 2) + P * k
                            last = nc.tensor.transpose(ps[:, P * k:P * (k + 1)], SQ[:, c:c + P], ident[:, :])
                        last.then_inc(t_xt.sem, 1)
                    elif kind == "V":
                        c = slice(P * u, P * (u + 1))
                        terms = [t for k in range(KT) for t in (
                            (XH[:, k, c], WH["v"][:, k, :]), (XH[:, k, c], WL["v"][:, k, :]), (XL[:, k, c], WH["v"][:, k, :]))]
                        products(ps[:, :], terms).then_inc(t_v.sem, 1)
                    elif kind == "P":
                        w, g, h = "kq"[u // NG], u % NG, stage[2]
                        o, c = slice(P * g, P * (g + 1)), slice(HALF * h, HALF * (h + 1))
                        if u == 0 and h == 0:
                            pe.wait_ge(v_xlo.sem, v_xlo.nth(j, TT))
                        terms = [t for k in range(KT) for t in (
                            (WH[w][:, k, o], XH[:, k, c]), (WL[w][:, k, o], XH[:, k, c]), (WH[w][:, k, o], XL[:, k, c]))]
                        products(ps[:, :], terms).then_inc(t_p.sem, 1)
                    elif kind == "N":
                        pe.wait_ge(a_p.sem, a_p.nth(j, 4 * u + 4))
                        for c in range(4):
                            last = mm(ps[DH * c:DH * (c + 1), 0:256], NP_[:, :], SQ[:, 256 * c:256 * (c + 1)],
                                      start=True, stop=True, tile_position=(0, DH * c))
                        last.then_inc(t_n.sem, 1)
                    elif kind == "F":
                        r = stage[2]
                        if r == 0:
                            unit_lifted(pe, j, u)
                            norms_lifted(pe, j, u)
                        slot = ST[:, u % 2, :]
                        if u < NG:
                            for p in range(2):
                                a, b = L * p + P * r, L * (2 + p) + P * r
                                last = products(ps[:, 256 * p:256 * (p + 1)], [(slot[:, a:a + P], MA[:, :]),
                                                                              (slot[0:KK, b:b + P], MB[0:KK, p, :])])
                        else:
                            h, half = r % 4, r // 4
                            c = L * h + HALF * half
                            last = mm(ps[:, :], WQS[0:QK, h, :], slot[0:QK, c:c + HALF], start=True, stop=True)
                        last.then_inc(t_f.sem, 1)
                    elif kind == "G" and u < NG:
                        r, kv = stage[2], ND[u % 2]
                        pe.wait_ge(a_exp.sem, a_exp.nth(j, 8 * u + r + 1))
                        if r == 0:
                            if u == 0:
                                pe.wait_ge(a_v.sem, a_v.nth(j, TT))
                            if u < 2:
                                pe.wait_ge(v_a.sem, v_a.nth(j, u - 1))
                            else:
                                pe.wait_ge(a_kc.sem, a_kc.nth(j, 3 * (u - 1)))
                        for h in range(HG):
                            rows = slice(DH * h, DH * (h + 1))
                            mm(kv[rows, 0:M + 1], VA[:, r, P * u + DH * h:P * u + DH * (h + 1)], FE[:, r % 4, h, :],
                               start=(r == 0), stop=(r == 7), tile_position=(0, DH * h), skip_group_check=True)
                        for h in range(HG):
                            rows = slice(DH * h, DH * (h + 1))
                            last = mm(kv[rows, 2 * M:3 * M], ones[:, 0:DH], FE[:, r % 4, h, 0:M],
                                      start=False, stop=(r == 7), tile_position=(0, DH * h), skip_group_check=True)
                        last.then_inc(t_g.sem, 1)
                    elif kind == "KVT":
                        pe.wait_ge(a_kc.sem, a_kc.nth(j, 3 * u + 3))
                        nc.tensor.transpose(ps[:, 0:P], KVT[:, 0:M], ident[:, :])
                        nc.tensor.transpose(ps[:, P:2 * P], KVT[:, M:2 * M], ident[:, :]).then_inc(t_kvt.sem, 1)
                    elif kind == "G":
                        g, h, half, n = u - NG, stage[2] % 4, stage[2] // 4, 8 * u + stage[2]
                        pe.wait_ge(a_exp.sem, a_exp.nth(j, n + 1))
                        if h == 0:
                            if half == 0:
                                pe.wait_ge(v_kvc.sem, v_kvc.nth(j, g + 1))
                            if g == 0:
                                pe.wait_ge(a_kc.sem, a_kc.nth(j, 3 * (half + 3)))
                            else:
                                pe.wait_ge(v_a.sem, v_a.nth(j, 2 * (g - 1) + half + 1))
                            pe.wait_ge(a_den.sem, a_den.nth(j, 2 * g + half))
                        rows, q = slice(DH * h, DH * (h + 1)), FE[:, n % 4, :, 0:M]
                        mm(DN[rows, :], KVS[:, g, P + DH * h:P + DH * (h + 1)], q, start=True, stop=True, tile_position=(0, DH * h))
                        mm(ND[half][rows, :], KVS[:, g, DH * h:DH * (h + 1)], q, start=True, stop=True,
                           tile_position=(0, DH * h)).then_inc(t_g.sem, 1)
                    elif kind == "O":
                        pe.wait_ge(v_alo.sem, v_alo.nth(j, u + 1))
                        ah = ST[:, 1, D * (u % 2):D * (u % 2 + 1)]
                        al = ST[:, 1, 1024 + D * (u % 2):1024 + D * (u % 2 + 1)]
                        terms = [t for k in range(KT) for t in (
                            (ah[:, P * k:P * (k + 1)], WH["o"][:, k, :]), (ah[:, P * k:P * (k + 1)], WL["o"][:, k, :]),
                            (al[:, P * k:P * (k + 1)], WH["o"][:, k, :]))]
                        products(ps[:, :], terms).then_inc(t_o.sem, 1)
                    elif kind == "YT":
                        pe.wait_ge(a_y.sem, a_y.nth(j, u + 1))
                        for k in range(KT):
                            last = nc.tensor.transpose(ps[:, P * k:P * (k + 1)], XR[:, u % 4, P * k:P * (k + 1)], ident[:, :])
                        last.then_inc(t_yt.sem, 1)
                    elif kind == "FF":
                        pe.wait_ge(v_ylo.sem, v_ylo.nth(j, u + 1))
                        terms = [t for k in range(KT) for t in (
                            (ST[:, 1, 2048 + P * k:2048 + P * (k + 1)], WT3[:, k, :]),
                            (ST[:, 1, 2560 + P * k:2560 + P * (k + 1)], WT3[:, k, :]))]
                        products(ps[:, :], terms).then_inc(t_ff.sem, 1)

            batches(pe, program)


_INS = ["L0_attn_x", "L0_attn_Wq", "L0_attn_bq", "L0_attn_Wk", "L0_attn_bk", "L0_attn_Wv", "L0_attn_bv",
        "L0_attn_Wo", "L0_attn_bo", "L0_attn_orf", "L0_ffn_weight"]


def kernel(**inputs):
    import numpy as _np
    import concourse.bacc as _bacc
    from concourse import mybir as _mybir
    from concourse.bass_utils import run_bass_kernel_spmd as _run

    nc = _bacc.Bacc("TRN2", target_bir_lowering=False, num_devices=1)
    arrays, args = {}, []
    for name in _INS:
        a = _np.ascontiguousarray(inputs[name])
        arrays[f"in_{name}"] = a
        args.append(nc.dram_tensor(f"in_{name}", a.shape, _mybir.dt.from_np(a.dtype), kind="ExternalInput").ap())
    args.append(nc.dram_tensor("out_0", (B, L, D), _mybir.dt.float32, kind="ExternalOutput").ap())
    attention_kernel(nc, *args)
    r = _run(nc, [arrays], core_ids=[0])
    return r.results[0]["out_0"]
```

```python
import math
from contextlib import ExitStack

import concourse.bass as bass
from concourse import mybir

F32, F32R = mybir.dt.float32, mybir.dt.float32r
ACT, ALU = mybir.ActivationFunctionType, mybir.AluOpType

B, L, D, H, DH, M = 8, 1024, 512, 16, 32, 128
P = 128
KT = D // P
TT = L // P
HG = 4
NG = H // HG
NU = 2 * NG
HALF = L // 2
EPS, LN_EPS, W_EPS = 1e-6, 1e-5, 1e-5
C_EXP = DH ** -0.25
A_SQ = math.sqrt(1.0 / (2.0 * math.sqrt(DH)) / C_EXP)
NR = 2 * HG
QK = 3 * DH + NR
KK = 2 * DH + NR


def unit_stages(u, more):
    ahead = u + 2 < NU
    p = [[("P", u + 2, h, part)] if ahead else [] for h in range(2) for part in range(2)]
    norms = [("N", u + 1)] if u + 1 < NU else []
    last_keys = [("G", u - 1, 7)] if 0 < u <= NG else []
    if u < NG:
        seq = [("F", u, 0), ("F", u, 1)] + p[0] + last_keys + norms + p[1] + [("G", u, 0)]
        for r in range(1, 7):
            seq += [("L", u + 2, 0)] if r == 6 else []
            seq += [("F", u, r + 1)] + ([("S", u + 2, 0)] if r == 1 else [])
            seq += p[2] if r == 3 else p[3] if r == 5 else []
            seq += [("G", u, r)] + ([("KVT", u - 1)] if u and r == 2 else [])
        return seq + [("S", u + 2, 1), ("L", u + 2, 1)]
    splits = [[("S", u + 2, 0)], [("L", u + 2, 0), ("S", u + 2, 1), ("L", u + 2, 1)]] if ahead else [[], []]
    xt = [[], []]
    if more and u == NU - 2:
        xt = [[("XT", t) for t in range(3)], [("XT", t) for t in range(3, 6)]]
    elif more and u == NU - 1:
        xt = [[("XT", 6), ("XT", 7)], []]
        p = [[], [], [("P", 0, 0, 0), ("P", 0, 0, 1)], [("P", 0, 1, 0), ("P", 0, 1, 1)]]
        splits = [[], [("S", 0, 0), ("L", 0, 0), ("S", 0, 1), ("L", 0, 1)]]
    seq = [("F", u, 0), ("F", u, 1)] + p[0] + last_keys + norms
    seq += [("F", u, 2), ("F", u, 3)] + p[1] + splits[0] + [("GG", u, 0)] + xt[0] + [("R", u, 0)]
    seq += [("F", u, 4), ("F", u, 5)] + p[2] + [("F", u, 6), ("F", u, 7)] + ([("KVT", NG - 1)] if u == NG else [])
    seq += [("A", 0), ("A", 1)] if u == NU - 1 else []
    return seq + p[3] + splits[1] + [("GG", u, 1)] + xt[1] + [("R", u, 1)]


def output_stages(more):
    def also(*stages):
        return list(stages) if more else []

    seq = [("O", 0), ("A", 2), ("O", 1)] + also(("N", 0))
    seq += [("A", 3), ("O", 2), ("YT", 0)] + also(("V", 0)) + [("FF", 0), ("YT", 1)]
    for t in range(3, TT):
        seq += ([("A", t + 1)] if t + 1 < TT else []) + [("O", t), ("ST", t - 3)]
        seq += [("FF", t - 2)] + also(("V", t - 2)) + [("YT", t - 1)]
    seq += also(("V", TT - 2)) + [("ST", TT - 3), ("FF", TT - 2)] + also(("P", 1, 0, 0)) + [("YT", TT - 1)]
    seq += also(("P", 1, 0, 1), ("S", 1, 0), ("L", 1, 0)) + [("FF", TT - 1)]
    seq += also(("V", TT - 1)) + [("ST", TT - 2)]
    return seq + also(("P", 1, 1, 0), ("P", 1, 1, 1), ("S", 1, 1), ("L", 1, 1)) + [("ST", TT - 1)]


PROLOGUE = [("XT", t) for t in range(TT)] + [("V", t) for t in range(TT - 1)]
PROLOGUE += [("P", 0, 0, 0), ("P", 0, 0, 1), ("S", 0, 0), ("L", 0, 0), ("P", 0, 1, 0), ("P", 0, 1, 1), ("S", 0, 1),
             ("L", 0, 1), ("N", 0), ("P", 1, 0, 0), ("P", 1, 0, 1), ("S", 1, 0), ("L", 1, 0), ("V", TT - 1),
             ("P", 1, 1, 0), ("P", 1, 1, 1), ("S", 1, 1), ("L", 1, 1)]
BODY = [s for u in range(NU) for s in unit_stages(u, True)] + output_stages(True)
LAST = [s for u in range(NU) for s in unit_stages(u, False)] + output_stages(False)

RING = {"V": "pj", "P": "pj", "O": "pj", "FF": "pj", "F": "ft", "XT": "ft", "YT": "ft", "N": "nb", "KVT": "nb"}
RING_SIZE = {"pj": 2, "ft": 2, "nb": 1}


def bank_uses(seq, before):
    uses = {ring: list(before[ring]) for ring in RING_SIZE}
    out = []
    for n, stage in enumerate(seq):
        ring = RING.get(stage[0])
        if stage[0] in "SL":
            out.append((next(bank for s, (bank, _) in zip(seq, out) if s == ("P", *stage[1:], 0)), None))
            continue
        if ring is None:
            out.append((None, None))
            continue
        size = RING_SIZE[ring]
        mine = uses[ring]
        if stage[0] == "P" and stage[3]:
            out.append((out[mine[-1][0]][0], None))
            continue
        old = mine[-size] if len(mine) >= size else None
        out.append(((len(mine) - len(before[ring])) % size, old))
        mine.append((n, stage))
    return out


def tail(seq):
    out = {}
    for ring, size in RING_SIZE.items():
        mine = [(None, s) for s in seq if RING.get(s[0]) == ring and not (s[0] == "P" and s[3])]
        out[ring] = mine[-size:]
    return out


def attention_kernel(nc, x, Wq, bq, Wk, bk, Wv, bv, Wo, bo, orf, wff, out):
    x_tiles = x.rearrange("b (t p) d -> b t p d", p=P)
    out_tiles = out.rearrange("b (t p) d -> b t p d", p=P)

    ctx = ExitStack()
    with ctx:
        def sb(name, shape, dt=F32):
            return ctx.enter_context(nc.sbuf_tensor(name, shape, dt))

        def sem(name):
            return ctx.enter_context(nc.semaphore(name))

        WH = {w: sb(f"W{w}_hi", [P, KT, D], F32R) for w in "qkvo"}
        WL = {w: sb(f"W{w}_lo", [P, KT, D], F32R) for w in "qkvo"}
        WT3 = sb("W_ternary", [P, KT, D], F32R)
        XH, XL = sb("x_hi", [P, KT, L], F32R), sb("x_lo", [P, KT, L], F32R)
        VA = sb("values_then_attention", [P, TT, D])
        ST = sb("stacks", [P, 2, 4 * L], F32R)
        EH, EL = sb("unit_hi", [P, 2, L], F32R), sb("unit_lo", [P, L], F32R)
        SQ = sb("squares_then_x", [P, L])
        FE = sb("features", [P, 4, HG, M + 1])
        XR = sb("rows", [P, 4, D])
        BO = sb("out_bias", [P, D])
        ident = sb("ident", [P, P])
        WQS = sb("orf_query", [P, HG, M], F32R)
        MA = sb("orf_key_a", [P, 2 * M], F32R)
        MB = sb("orf_key_b", [P, 2, 2 * M], F32R)
        NP_ = sb("norm_columns", [P, DH])
        ones = sb("ones", [P, P])
        KVS = sb("kv_ksum", [P, NG, 2 * P])
        KVT = sb("kv_ksum_t", [P, 2 * P])
        NH, NN = sb("norm_hi", [P, 2 * P], F32R), sb("norm_rows", [P, 2 * P], F32R)
        DR = sb("den", [P, 2, HALF])
        cols = sb("cols", [P, 128])

        def col(a, n=1):
            return cols[:, a:a + n]

        BC, ABC, BVC = col(0, NU), col(NU, NU), col(2 * NU, KT)
        NEGM, EPSL, EXPO, EV = col(20), col(21), col(22), col(23)
        WSUM, SC, HS, NHS = col(24), col(25), col(26), col(27)
        RSUM, CC = col(28, 2 * NG), col(36, 2 * NG)
        stats = sb("stats", [P, 2, 4, 12])

        def ln(kind, t, a, n=1):
            return stats[:, kind, t % 4, a:a + n]

        PS = [ctx.enter_context(nc.psum_tensor(f"ps{i}", [P, 512], F32)) for i in range(8)]
        BANKS = {"pj": PS[0:2], "ft": PS[2:4], "nb": PS[4:5]}
        ND, DN = PS[5:7], PS[7]

        class Signal:

            def __init__(self, name, per, credit=0, step=1):
                self.sem, self.per, self.credit, self.step = sem(name), per, credit, step

            def nth(self, batch, k):
                return batch[0] * (self.per * self.step) + (self.credit + k + batch[1] * self.per) * self.step

        t_xt, t_v, t_p = Signal("xt_done", TT), Signal("v_done", TT), Signal("p_done", 2 * NU)
        t_n, t_kvt = Signal("n_done", NU, 1), Signal("kvt_done", NG, 1)
        t_f, t_g, t_gg = Signal("f_done", 8 * NU, 9), Signal("g_done", 8 * NG), Signal("gg_done", 2 * NG, 1)
        t_o, t_yt, t_ff = Signal("o_done", TT), Signal("yt_done", TT), Signal("ff_done", TT, 1)
        a_xhi, a_v, a_p = Signal("x_hi_ready", TT), Signal("v_ready", TT), Signal("unit_hi_sq_ready", 4 * NU)
        a_exp, a_kc = Signal("features_ready", 8 * NU), Signal("kv_copied", 3 * NG)
        a_den, a_ahi = Signal("den_copied", 2 * NG, 1), Signal("a_hi_ready", TT)
        a_y, a_yhi, a_out = Signal("y_ready", TT), Signal("y_hi_ready", TT), Signal("out_ready", TT)
        v_xlo, v_plo, v_n = Signal("x_lo_ready", TT), Signal("unit_lo_ready", 2 * NU), Signal("norms_ready", 2 * NU)
        v_ks = Signal("features_added", 7 * NG)
        v_kvc, v_c = Signal("kv_ready", NG), Signal("eps_sums_ready", NG)
        v_rc, v_a = Signal("reciprocal_ready", 2 * NG), Signal("attention_ready", 2 * NG, 2)
        v_alo, v_ylo = Signal("a_lo_ready", TT, TT), Signal("y_lo_ready", TT, 2)
        v_ln = [Signal("ln1_steps", 5 * TT, 1), Signal("ln2_steps", 5 * TT, 4)]
        g_xb = Signal("x_plus_bias_ready", TT)
        g_ln = [Signal("ln1_scale_ready", 2 * TT), Signal("ln2_scale_ready", 2 * TT)]
        d_xl = [Signal(f"x_loaded{t}", 1, 0, 16) for t in range(TT)]
        d_xr = [Signal(f"rows_loaded{t}", 1, 0, 16) for t in range(TT)]
        d_st = [Signal(f"rows_stored{s}", TT // 4, 1, 16) for s in range(4)]
        KEY_LIFTS, QUERY_LIFTS = 10, 12
        lifted = [Signal(f"stack_lifted{s}", 2 * (KEY_LIFTS + QUERY_LIFTS), 1, 16) for s in range(2)]
        n_lifted = [Signal("norms_lifted_even", 4 * (NG - 1), 0, 16), Signal("norms_lifted_odd", 4 * NG, 0, 16)]
        n_first = Signal("norms_lifted_first", 4, 0, 16)

        def lifts(u):
            n = u // 2 + 1
            return KEY_LIFTS * min(n, 2) + QUERY_LIFTS * max(n - 2, 0)

        def unit_lifted(eng, j, u):
            if u < 0:
                eng.wait_ge(lifted[u % 2].sem, lifted[u % 2].nth(j, 0))
            else:
                eng.wait_ge(lifted[u % 2].sem, lifted[u % 2].nth(j, lifts(u)))

        def norms_lifted(eng, j, u):
            if u < 0:
                if j[1]:
                    eng.wait_ge(n_lifted[1].sem, n_lifted[1].nth(j, 0))
            elif u == 0:
                eng.wait_ge(n_first.sem, n_first.nth(j, 4))
            else:
                eng.wait_ge(n_lifted[u % 2].sem, n_lifted[u % 2].nth(j, 4 * ((u + 1) // 2)))

        def lift_norms(queue, wait, sig, j, u):
            slot = ST[:, u % 2, :].bitcast(F32)
            wait(v_n.sem, v_n.nth(j, 2 * u + 2))
            for c in range(4):
                src = NN[DH * c:DH * c + NR, :].bitcast(F32).unsqueeze(1)
                if u < NG:
                    dst = slot[2 * DH:2 * DH + NR, 2 * L:4 * L].rearrange("p (a t) -> p a t", a=2)
                    n = 2
                else:
                    dst = slot[3 * DH:3 * DH + NR, :].rearrange("p (a t) -> p a t", a=HG)
                    n = HG
                queue.dma_start(dst[:, :, 256 * c:256 * (c + 1)], src.broadcast_to([NR, n, 256])).then_inc(sig.sem, 16)

        s_ld, s_k, s_pe, s_act, s_dve, s_pool = (sem(n) for n in (
            "setup_loaded", "setup_consts", "setup_pe", "setup_act", "setup_dve", "setup_pool"))
        s_wlo, s_chain, s_bv = sem("setup_w_lo"), sem("setup_chain"), sem("setup_bv")
        s_go, s_pin = sem("setup_finished"), sem("carries_a_wait")
        s_ld2 = [sem(f"setup_w{n}") for n in range(5)]

        WS = [VA[:, 4 * n:4 * n + 4, :] for n in range(2)]
        sources = [Wq, Wk, Wv, Wo, wff]
        orf_rep = DR[:, 1, 0:P]
        bv_rep = DR[:, 0, :]
        lo_rows = FE[:, 1, 0, 0:4 * HG]

        def x_stage(t):
            return XR[:, t, :] if t < 4 else SQ[:, D * (t % 2):D * (t % 2 + 1)]

        def x_rows(t):
            return XR[:, t, :].rearrange("p (a m) -> p a m", a=HG) if t < 4 else FE[:, t - 4, :, 0:M]

        def old_bank(stage, j):
            kind, k = stage[0], stage[1]
            if kind == "V":
                return a_v, a_v.nth(j, k + 1)
            if kind == "P":
                return v_plo, v_plo.nth(j, 2 * k + stage[2] + 1)
            if kind == "O":
                return v_ln[0], v_ln[0].nth(j, 5 * k + 1)
            if kind == "FF":
                return v_ln[1], v_ln[1].nth(j, 5 * k + 1)
            if kind == "F":
                return a_exp, a_exp.nth(j, 8 * k + stage[2] + 1)
            if kind == "XT":
                return v_xlo, v_xlo.nth(j, k + 1)
            if kind == "YT":
                return v_ylo, v_ylo.nth(j, k + 1)
            if kind == "N":
                return v_n, v_n.nth(j, 2 * k + 2)
            return v_kvc, v_kvc.nth(j, k + 1)

        def looks_ahead(stage):
            return stage[0] in ("XT", "V") or stage[:2] == ("N", 0) or (stage[0] in "PSL" and stage[1] < 2)

        none = {ring: [] for ring in RING_SIZE}
        BANKING = {id(PROLOGUE): bank_uses(PROLOGUE, none), id(BODY): bank_uses(BODY, tail(BODY)),
                   id(LAST): bank_uses(LAST, tail(BODY))}

        def steps(seq, j):
            for n, (stage, (bank, old)) in enumerate(zip(seq, BANKING[id(seq)])):
                mine = (j, 1) if seq is BODY and looks_ahead(stage) else (j, 0)
                if old is not None:
                    m, prev = old
                    if m is None:
                        old = (prev, (j, 0 if looks_ahead(prev) else -1))
                    else:
                        old = (prev, (j, 1 if seq is BODY and looks_ahead(prev) else 0))
                yield stage, mine, (None if bank is None else BANKS[RING.get(stage[0], "pj")][bank]), old

        def batches(eng, program):
            program(PROLOGUE, 0)
            with eng.Fori(0, B - 1) as i:
                program(BODY, i)
            program(LAST, B - 1)

        block = ctx.enter_context(nc.Block())

        @block.sync
        def _(sp):
            sp.dma_start(BC[:, 0:NG], bk.rearrange("(g p) -> p g", p=P), allow_slow_non_contiguous=True).then_inc(s_ld, 16)
            sp.dma_start(BC[:, NG:NU], bq.rearrange("(g p) -> p g", p=P), allow_slow_non_contiguous=True).then_inc(s_ld, 16)
            sp.dma_start(BVC, bv.rearrange("(g p) -> p g", p=P), allow_slow_non_contiguous=True).then_inc(s_ld, 16)
            sp.dma_start(BO[:, :], bo.unsqueeze(0).broadcast_to([P, D])).then_inc(s_ld, 16)
            for r in range(4):
                sp.dma_start(orf_rep[:, DH * r:DH * (r + 1)], orf).then_inc(s_ld, 16)
            for n, w in enumerate(sources):
                if n >= 2:
                    sp.wait_ge(s_pe, 4 * (n - 1) + 1)
                sp.dma_start(WS[n % 2], w.rearrange("(a p) i -> p a i", p=P)).then_inc(s_ld2[n], 16)
            for sig in lifted:
                sp.sem_inc(sig.sem, sig.credit * sig.step)

            def wait(semaphore, value):
                sp.wait_ge(semaphore, value)
                sp.sem_inc(s_pin, 1)

            def load_x(j, t):
                sp.dma_start(x_stage(t), x_tiles[j[0] + j[1], t]).then_inc(d_xl[t].sem, 16)

            def load_rows(j, t, ahead=False):
                if t == 0 and ahead:
                    wait(t_xt.sem, t_xt.nth((j[0], 1), 4))
                elif t < 4 and not ahead:
                    wait(d_st[t].sem, d_st[t].nth(j, 0))
                elif t == 4:
                    wait(t_gg.sem, t_gg.nth(j, 2 * NG))
                sp.dma_start(x_rows(t), x_tiles[j[0] + j[1], t].rearrange("p (a m) -> p a m", a=HG))\
                    .then_inc(d_xr[t].sem, 16)

            def program(seq, i):
                if seq is PROLOGUE:
                    for t in range(4):
                        load_x((0, 0), t)
                for stage, j, _, _ in steps(seq, i):
                    kind, u = stage[0], stage[1]
                    if kind == "O" and u == 0:
                        for t in range(4, TT):
                            load_rows(j, t)
                    elif kind == "L" and stage[2] == 1:
                        slot = ST[:, u % 2, :].bitcast(F32)
                        hi, lo, sig = EH[:, u % 2, :].bitcast(F32), EL[:, :].bitcast(F32), lifted[u % 2]
                        wait(t_f.sem, t_f.nth(j, 8 * (u - 1)))
                        if u == 1:
                            wait(t_ff.sem, t_ff.nth(j, 0))
                        wait(a_p.sem, a_p.nth(j, 4 * u + 3))
                        for h in range(HG):
                            src = hi[DH * h:DH * (h + 1), :]
                            if u < NG:
                                r, c = 2 * DH * (h % 2), L * (h // 2)
                                sp.dma_start(slot[r:r + DH, c:c + L], src).then_inc(sig.sem, 16)
                            else:
                                sp.dma_start(slot[0:DH, L * h:L * (h + 1)], src).then_inc(sig.sem, 16)
                                sp.dma_start(slot[2 * DH:3 * DH, L * h:L * (h + 1)], src).then_inc(sig.sem, 16)
                        if u < NG:
                            for p in range(2):
                                sp.dma_start(slot[0:2 * DH, L * (2 + p):L * (3 + p)],
                                             hi[2 * DH * p:2 * DH * (p + 1), :]).then_inc(sig.sem, 16)
                        wait(v_plo.sem, v_plo.nth(j, 2 * u + 2))
                        for h in range(HG):
                            r, c = (2 * DH * (h % 2) + DH, L * (h // 2)) if u < NG else (DH, L * h)
                            sp.dma_start(slot[r:r + DH, c:c + L], lo[DH * h:DH * (h + 1), :]).then_inc(sig.sem, 16)
                    elif kind == "N" and u == 0:
                        lift_norms(sp, wait, n_first, j, 0)
                    elif kind == "N" and u == NU - 2 and seq is BODY:
                        for t in range(4):
                            wait(d_st[t].sem, d_st[t].nth(j, 0))
                            load_x((i, 1), t)
                    elif kind == "XT" and u == 4 and seq is BODY or kind == "N" and u == NU - 1 and seq is LAST:
                        for t in range(4):
                            load_rows((i, 0), t, seq is BODY)

            batches(sp, program)

        @block.gpsimd
        def _(pool):
            filled = [1]

            def fill_where(t, base, pattern, cm, fill):
                pool.wait_ge(s_k, filled[0])
                filled[0] += 1
                nc.gpsimd.affine_select(out=t, in_=t, compare_op=ALU.not_equal, fill=fill, base=base,
                                        pattern=pattern, channel_multiplier=cm).then_inc(s_k, 1)

            nc.gpsimd.memset(ident[:, :], 0.0)
            nc.gpsimd.memset(ones[:, :], 1.0)
            nc.gpsimd.memset(NP_[:, :], 0.0)
            nc.gpsimd.memset(lo_rows, 0.0)
            nc.gpsimd.memset(FE[:, 2, :, :], 0.0)
            nc.gpsimd.memset(EXPO, -0.5)
            nc.gpsimd.memset(EPSL, EPS * L)
            for t in (WQS, MA, MB):
                last = nc.gpsimd.memset(t[:].bitcast(F32), 0.0)
            last.then_inc(s_k, 1)
            fill_where(ident[:, :], 0, [[-1, P]], 1, 1.0)
            pool.wait_ge(s_k, filled[0])
            filled[0] += 1
            for h in range(HG):
                nc.gpsimd.memset(NP_[DH * h:DH * (h + 1), h:h + 1], 1.0)
                last = nc.gpsimd.memset(NP_[DH * h:DH * (h + 1), HG + h:HG + h + 1], 1.0)
            last.then_inc(s_k, 1)
            fill_where(lo_rows.rearrange("p (a b) -> p a b", a=4), -HG, [[-DH, 4], [-1, HG]], 1, -1.0)
            q_rows = FE[3 * DH:QK, 2, :, 0:M]
            fill_where(q_rows, 0, [[-1, HG], [0, M]], 1, -1.0)
            fill_where(q_rows, -HG, [[-1, HG], [0, M]], 1, -1.0)
            k_rows = FE[2 * DH:KK, 2, :, 0:M]
            fill_where(k_rows, 0, [[-1, HG], [0, M]], 1, -1.0)
            fill_where(k_rows, -HG, [[-1, HG], [0, M]], 1, -1.0)
            pool.wait_ge(s_k, filled[0])
            pool.wait_ge(s_dve, 1)
            pool.wait_ge(s_pe, 1)
            nc.gpsimd.memset(FE[:, :, :, M:M + 1], 1.0).then_inc(s_pool, 1)

            def layer_scale(k, j, t):
                pool.wait_ge(v_ln[k].sem, v_ln[k].nth(j, 5 * t + 5))
                nc.gpsimd.tensor_tensor(ln(k, t, 10), ln(k, t, 8), EXPO, ALU.pow).then_inc(g_ln[k].sem, 1)
                pool.wait_ge(g_ln[k].sem, g_ln[k].nth(j, 2 * t + 1))
                nc.gpsimd.tensor_tensor(ln(k, t, 11), ln(k, t, 9), ln(k, t, 10), ALU.mult).then_inc(g_ln[k].sem, 1)

            def wait(semaphore, value):
                pool.wait_ge(semaphore, value)
                pool.sem_inc(s_pin, 1)

            def load_x(j, t):
                pool.dma_start(x_stage(t), x_tiles[j[0] + j[1], t]).then_inc(d_xl[t].sem, 16)

            def program(seq, i):
                if seq is PROLOGUE:
                    load_x((0, 0), 4)
                    load_x((0, 0), 5)
                for stage, j, _, _ in steps(seq, i):
                    kind, t = stage[0], stage[1]
                    if kind == "XT" and 4 <= t < 6:
                        wait(t_xt.sem, t_xt.nth(j, t + 1))
                        load_x(j, t + 2)
                    elif kind == "N" and t > 0:
                        if t == NU - 1 and seq is BODY:
                            wait(t_n.sem, t_n.nth(j, NU))
                            load_x((i, 1), 4)
                            load_x((i, 1), 5)
                        lift_norms(pool, wait, n_lifted[t % 2], j, t)
                    elif kind == "A":
                        pool.wait_ge(d_xr[t].sem, d_xr[t].nth(j, 1))
                        nc.gpsimd.tensor_tensor(x_rows(t), x_rows(t), BO[:, :].rearrange("p (a m) -> p a m", a=HG), ALU.add).then_inc(g_xb.sem, 1)
                    elif kind == "O":
                        layer_scale(0, j, t)
                    elif kind == "FF":
                        layer_scale(1, j, t)

            pool.wait_ge(s_dve, 4)
            batches(pool, program)

        @block.scalar
        def _(act):
            for sig in (a_den,):
                act.sem_inc(sig.sem, sig.credit)
            for sig in d_st:
                act.sem_inc(sig.sem, sig.credit * sig.step)
            for n in range(4):
                w = "qkvo"[n]
                for k in range(KT):
                    act.wait_ge(s_pe, 4 * n + k + 2)
                    nc.scalar.activation(WH[w][:, k, :], PS[(4 * n + k) % 4][:, :], ACT.Copy).then_inc(s_act, 1)
            act.wait_ge(s_ld2[4], 16)
            nc.scalar.activation(WS[1].rearrange("p a i -> p (a i)"), WS[0].rearrange("p a i -> p (a i)"), ACT.Abs,
                                 accum_out=WSUM).then_inc(s_act, 1)
            act.wait_ge(s_go, 1)

            def program(seq, i):
                for stage, j, ps, _ in steps(seq, i):
                    kind, u = stage[0], stage[1]
                    if kind == "XT":
                        act.wait_ge(t_xt.sem, t_xt.nth(j, u + 1))
                        nc.scalar.activation(XH[:, :, P * u:P * (u + 1)], ps[:, :].rearrange("p (k c) -> p k c", k=KT),
                                             ACT.Copy).then_inc(a_xhi.sem, 1)
                    elif kind == "V":
                        act.wait_ge(t_v.sem, t_v.nth(j, u + 1))
                        act.wait_ge(v_alo.sem, v_alo.nth(j, u + 1 - TT))
                        nc.scalar.activation(VA[:, u, :], ps[:, :], ACT.Copy).then_inc(a_v.sem, 1)
                    elif kind == "S":
                        h, half = stage[2], slice(HALF * stage[2], HALF * (stage[2] + 1))
                        act.wait_ge(t_p.sem, t_p.nth(j, 2 * u + h + 1))
                        if h == 0:
                            unit_lifted(act, j, u - 2)
                        nc.scalar.activation(EH[:, u % 2, half], ps[:, :], ACT.Identity, bias=BC[:, u:u + 1]).then_inc(a_p.sem, 1)
                        if h == 0:
                            act.wait_ge(t_n.sem, t_n.nth(j, u))
                        nc.scalar.activation(SQ[:, half], ps[:, :], ACT.Square, bias=ABC[:, u:u + 1],
                                             scale=A_SQ).then_inc(a_p.sem, 1)
                    elif kind == "F":
                        n = 8 * u + stage[2]
                        act.wait_ge(t_f.sem, t_f.nth(j, n + 1))
                        if n == 0:
                            act.wait_ge(v_ln[0].sem, v_ln[0].nth(j, 0))
                        if n < 4 or n >= 8 * NG + 4:
                            act.wait_ge(t_gg.sem, t_gg.nth(j, max(n - 8 * NG, 0) // 4))
                        else:
                            act.wait_ge(t_g.sem, t_g.nth(j, n - 3))
                            act.wait_ge(v_ks.sem, v_ks.nth(j, 7 * ((n - 4) // 8) + max((n - 4) % 8, 1)))
                        nc.scalar.activation(FE[:, n % 4, :, 0:M], ps[:, :].rearrange("p (a m) -> p a m", a=HG),
                                             ACT.Exp, scale=C_EXP).then_inc(a_exp.sem, 1)
                    elif kind == "G" and stage[2] == 7:
                        kv = ND[u % 2]
                        act.wait_ge(t_g.sem, t_g.nth(j, 8 * u + 8))
                        nc.scalar.activation(EV, kv[:, M:M + 1], ACT.Copy, scale=EPS).then_inc(a_kc.sem, 1)
                        act.wait_ge(t_kvt.sem, t_kvt.nth(j, u))
                        act.wait_ge(a_kc.sem, a_kc.nth(j, 3 * u + 1))
                        nc.scalar.activation(KVT[:, 0:M], kv[:, 0:M], ACT.Identity, bias=EV,
                                             accum_out=RSUM[:, 2 * u:2 * u + 1]).then_inc(a_kc.sem, 1)
                        nc.scalar.activation(KVT[:, M:2 * M], kv[:, 2 * M:3 * M], ACT.Identity, bias=EPSL,
                                             accum_out=RSUM[:, 2 * u + 1:2 * u + 2]).then_inc(a_kc.sem, 1)
                    elif kind == "GG":
                        g, h = u - NG, stage[2]
                        act.wait_ge(t_gg.sem, t_gg.nth(j, 2 * g + h + 1))
                        if h == 0:
                            act.wait_ge(v_c.sem, v_c.nth(j, g + 1))
                        act.wait_ge(v_a.sem, v_a.nth(j, 2 * g + h - 1))
                        nc.scalar.activation(DR[:, h, :], DN[:, :], ACT.Identity,
                                             bias=CC[:, 2 * g + 1:2 * g + 2]).then_inc(a_den.sem, 1)
                    elif kind == "A":
                        split_hi(j, u)
                    elif kind == "O" and u >= 1:
                        apply_norm(0, j, u - 1)
                    elif kind == "YT":
                        act.wait_ge(t_yt.sem, t_yt.nth(j, u + 1))
                        nc.scalar.activation(ST[:, 1, 2048:2560], ps[:, :], ACT.Copy).then_inc(a_yhi.sem, 1)
                    elif kind == "FF" and u == TT - 2:
                        apply_norm(0, j, u + 1)
                    elif kind == "ST":
                        apply_norm(1, j, u)
                        act.wait_ge(a_out.sem, a_out.nth(j, u + 1))
                        act.dma_start(out_tiles[j[0] + j[1], u], XR[:, u % 4, :]).then_inc(d_st[u % 4].sem, 16)

            def split_hi(j, t):
                act.wait_ge(v_a.sem, v_a.nth(j, 7 if t < 4 else 8))
                if t < 2:
                    act.wait_ge(t_f.sem, t_f.nth(j, 8 * NU))
                else:
                    act.wait_ge(t_o.sem, t_o.nth(j, t - 1))
                nc.scalar.activation(ST[:, 1, D * (t % 2):D * (t % 2 + 1)], VA[:, t, :], ACT.Copy).then_inc(a_ahi.sem, 1)

            def apply_norm(k, j, t):
                act.wait_ge(g_ln[k].sem, g_ln[k].nth(j, 2 * t + 2))
                row = XR[:, t % 4, :]
                nc.scalar.activation(row, row, ACT.Identity, scale=ln(k, t, 10), bias=ln(k, t, 11))\
                    .then_inc((a_y, a_out)[k].sem, 1)

            batches(act, program)
            for sig in d_st:
                act.wait_ge(sig.sem, sig.nth((B, 0), 0))

        @block.vector
        def _(dve):
            for sig in (v_a, v_alo, v_ylo, v_ln[0], v_ln[1]):
                dve.sem_inc(sig.sem, sig.credit)
            chain = [0]

            def link(ins):
                chain[0] += 1
                ins.then_inc(s_chain, 1)
                dve.wait_ge(s_chain, chain[0])

            dve.wait_ge(s_k, 8)
            nc.vector.reduce_sum(NEGM, lo_rows, axis=mybir.AxisListType.X)
            dve.wait_ge(s_ld, 16 * 8)
            nc.vector.tensor_scalar(ABC, BC, A_SQ, None, ALU.mult)
            for k in range(KT):
                last = nc.vector.tensor_scalar(bv_rep[:, P * k:P * (k + 1)], ones[:, :], BVC[:, k:k + 1], None, ALU.mult)
            last.then_inc(s_bv, 1)
            dve.wait_ge(s_pe, 1)
            wT = PS[7]
            for r in range(2):
                for h in range(HG):
                    nc.vector.tensor_copy(WQS[DH * r:DH * (r + 1), h, :], wT[DH * r:DH * (r + 1), 0:M])
            for r in range(4):
                a = r // 2
                nc.vector.tensor_copy(MA[DH * r:DH * (r + 1), M * a:M * (a + 1)], wT[DH * r:DH * (r + 1), 0:M])
            link(nc.vector.tensor_copy(EH[:, 0, 0:M], wT[:, 0:M]))
            for h in range(HG):
                r = slice(2 * DH, 3 * DH)
                nc.vector.tensor_tensor(WQS[r, h, :], wT[r, 0:M], EH[r, 0, 0:M].bitcast(F32), ALU.subtract)
            for p in range(2):
                for a in range(2):
                    r = slice(DH * a, DH * (a + 1))
                    nc.vector.tensor_tensor(MB[r, p, M * a:M * (a + 1)], wT[r, 0:M], EH[r, 0, 0:M].bitcast(F32), ALU.subtract)
            nc.vector.tensor_copy(WQS[3 * DH:QK, :, :], FE[3 * DH:QK, 2, :, 0:M])
            last = nc.vector.tensor_copy(MB[2 * DH:KK, :, :].rearrange("p a (b m) -> p (a b) m", b=2),
                                         FE[2 * DH:KK, 2, :, 0:M])
            last.then_inc(s_dve, 1)
            for n in range(4):
                w = "qkvo"[n]
                for k in range(KT):
                    dve.wait_ge(s_act, 4 * n + k + 1)
                    nc.vector.tensor_tensor(WL[w][:, k, :], PS[(4 * n + k) % 4][:, :], WH[w][:, k, :].bitcast(F32),
                                            ALU.subtract).then_inc(s_wlo, 1)
            dve.wait_ge(s_pe, 4 * 4 + 2)
            link(nc.vector.tensor_scalar(SC, PS[6][:, 0:1], 1.0 / (D * D), W_EPS, ALU.mult, ALU.max))
            link(nc.vector.tensor_scalar(HS, SC, 0.5, None, ALU.mult))
            link(nc.vector.tensor_scalar(NHS, SC, -0.5, None, ALU.mult))
            wf = WS[0].rearrange("p a i -> p (a i)")
            below = WS[1].rearrange("p a i -> p (a i)")
            link(nc.vector.tensor_scalar(below, wf, NHS, None, ALU.is_lt))
            nc.vector.scalar_tensor_tensor(out=wf, in0=wf, scalar=HS, in1=below, op0=ALU.is_gt,
                                           op1=ALU.subtract).then_inc(s_dve, 1)
            for k in range(KT):
                dve.wait_ge(s_pe, 4 * 4 + 3 + k)
                last = nc.vector.tensor_copy(WT3[:, k, :], PS[k][:, :])
            last.then_inc(s_dve, 1)
            dve.wait_ge(s_pe, 4 * 4 + 3 + KT)
            nc.vector.tensor_tensor(BO[:, :], PS[7][:, :], BO[:, :], ALU.add).then_inc(s_dve, 1)
            dve.wait_ge(s_pool, 1)
            dve.wait_ge(s_dve, 4)
            dve.sem_inc(s_go, 1)

            def layer_stats(k, j, t, source):
                sig, row, n = v_ln[k], XR[:, t % 4, :], 5 * t
                source().then_inc(sig.sem, 1)
                dve.wait_ge(sig.sem, sig.nth(j, n + 1))
                nc.vector.bn_stats(ln(k, t, 0, 6), row).then_inc(sig.sem, 1)
                dve.wait_ge(sig.sem, sig.nth(j, n + 2))
                dve.sem_inc(s_pin, 1)
                nc.vector.bn_aggr(ln(k, t, 6, 2), ln(k, t, 0, 6)).then_inc(sig.sem, 1)
                dve.wait_ge(sig.sem, sig.nth(j, n + 3))
                nc.vector.tensor_scalar(ln(k, t, 8), ln(k, t, 7), LN_EPS, None, ALU.add).then_inc(sig.sem, 1)
                nc.vector.tensor_scalar(ln(k, t, 9), ln(k, t, 6), -1.0, None, ALU.mult).then_inc(sig.sem, 1)

            def add_features(j, u, r):
                total, n = DR[:, u % 2, :].rearrange("p (a m) -> p a m", a=HG), 8 * u + r
                if r == 0:
                    return
                dve.wait_ge(a_exp.sem, a_exp.nth(j, n + 1))
                if r == 1:
                    if u < 2:
                        dve.wait_ge(v_a.sem, v_a.nth(j, 0))
                    else:
                        dve.wait_ge(t_g.sem, t_g.nth(j, 8 * (u - 1)))
                    ins = nc.vector.tensor_tensor(total, FE[:, 0, :, 0:M], FE[:, 1, :, 0:M], ALU.add)
                else:
                    dve.wait_ge(v_ks.sem, v_ks.nth(j, 7 * u + r - 1))
                    ins = nc.vector.tensor_tensor(total, total, FE[:, r % 4, :, 0:M], ALU.add)
                ins.then_inc(v_ks.sem, 1)

            def split_lo(j, t):
                dve.wait_ge(a_ahi.sem, a_ahi.nth(j, t + 1))
                nc.vector.tensor_tensor(ST[:, 1, 1024 + D * (t % 2):1024 + D * (t % 2 + 1)], VA[:, t, :],
                                        ST[:, 1, D * (t % 2):D * (t % 2 + 1)].bitcast(F32), ALU.subtract).then_inc(v_alo.sem, 1)

            def program(seq, i):
                for stage, j, ps, _ in steps(seq, i):
                    kind, u = stage[0], stage[1]
                    if kind == "XT":
                        dve.wait_ge(a_xhi.sem, a_xhi.nth(j, u + 1))
                        c = slice(P * u, P * (u + 1))
                        nc.vector.tensor_tensor(XL[:, :, c], ps[:, :].rearrange("p (k c) -> p k c", k=KT),
                                                XH[:, :, c].bitcast(F32), ALU.subtract).then_inc(v_xlo.sem, 1)
                    elif kind == "L":
                        h, half = stage[2], slice(HALF * stage[2], HALF * (stage[2] + 1))
                        dve.wait_ge(a_p.sem, a_p.nth(j, 2 * (2 * u + h) + 2))
                        if h == 0:
                            unit_lifted(dve, j, u - 1)
                        nc.vector.scalar_tensor_tensor(out=EL[:, half], in0=ps[:, :], scalar=BC[:, u:u + 1],
                                                       in1=EH[:, u % 2, half].bitcast(F32), op0=ALU.add,
                                                       op1=ALU.subtract).then_inc(v_plo.sem, 1)
                    elif kind == "N":
                        dve.wait_ge(t_n.sem, t_n.nth(j, u + 1))
                        norms_lifted(dve, j, u - 1)
                        nc.vector.tensor_copy(NH[:, :], ps[:, 0:256]).then_inc(v_n.sem, 1)
                        dve.wait_ge(v_n.sem, v_n.nth(j, 2 * u + 1))
                        nc.vector.scalar_tensor_tensor(out=NN[:, :], in0=NH[:, :].bitcast(F32), scalar=NEGM,
                                                       in1=ps[:, 0:256], op0=ALU.mult, op1=ALU.add).then_inc(v_n.sem, 1)
                    elif kind == "KVT":
                        dve.wait_ge(t_kvt.sem, t_kvt.nth(j, u + 1))
                        nc.vector.tensor_copy(KVS[:, u, :], ps[:, 0:256]).then_inc(v_kvc.sem, 1)
                    elif kind == "F" and u < NG:
                        add_features(j, u, stage[2])
                    elif kind == "G" and stage[2] == 7:
                        dve.wait_ge(a_kc.sem, a_kc.nth(j, 3 * u + 3))
                        nc.vector.tensor_scalar(CC[:, 2 * u:2 * u + 2], RSUM[:, 2 * u:2 * u + 2], EPS, None,
                                                ALU.mult).then_inc(v_c.sem, 1)
                    elif kind == "R":
                        g, h = u - NG, stage[2]
                        dve.wait_ge(a_den.sem, a_den.nth(j, 2 * g + h + 1))
                        nc.vector.reciprocal(DR[:, h, :], DR[:, h, :]).then_inc(v_rc.sem, 1)
                        dve.wait_ge(v_rc.sem, v_rc.nth(j, 2 * g + h + 1))
                        nc.vector.scalar_tensor_tensor(
                            out=VA[:, 4 * h:4 * h + 4, P * g:P * (g + 1)], in0=ND[h][:, :].rearrange("p (t c) -> p t c", t=4),
                            scalar=CC[:, 2 * g:2 * g + 1], in1=DR[:, h, :].rearrange("p (t c) -> p t c", t=4),
                            op0=ALU.add, op1=ALU.mult).then_inc(v_a.sem, 1)
                    elif kind == "A":
                        split_lo(j, u)
                    elif kind == "O":
                        dve.wait_ge(t_o.sem, t_o.nth(j, u + 1))
                        dve.wait_ge(g_xb.sem, g_xb.nth(j, u + 1))
                        if u >= 4:
                            dve.wait_ge(d_st[u % 4].sem, d_st[u % 4].nth(j, 1))
                        layer_stats(0, j, u, lambda: nc.vector.tensor_tensor(
                            XR[:, u % 4, :].rearrange("p (a m) -> p a m", a=HG), ps[:, :].rearrange("p (a m) -> p a m", a=HG),
                            x_rows(u), ALU.add))
                    elif kind == "YT":
                        dve.wait_ge(a_yhi.sem, a_yhi.nth(j, u + 1))
                        nc.vector.tensor_tensor(ST[:, 1, 2560:3072], ps[:, :], ST[:, 1, 2048:2560].bitcast(F32),
                                                ALU.subtract).then_inc(v_ylo.sem, 1)
                    elif kind == "FF":
                        dve.wait_ge(t_ff.sem, t_ff.nth(j, u + 1))
                        row = XR[:, u % 4, :]
                        layer_stats(1, j, u, lambda: nc.vector.scalar_tensor_tensor(
                            out=row, in0=ps[:, :], scalar=SC, in1=row, op0=ALU.mult, op1=ALU.add))

            batches(dve, program)

        @block.tensor
        def _(pe):
            for sig in (t_n, t_kvt, t_f, t_gg, t_ff):
                pe.sem_inc(sig.sem, sig.credit)
            mm = nc.tensor.matmul
            pe.wait_ge(s_k, 8)
            pe.wait_ge(s_ld, 16 * 8)
            nc.tensor.transpose(PS[7][:, 0:M], orf_rep, ident[:, :]).then_inc(s_pe, 1)
            for n in range(4):
                pe.wait_ge(s_ld2[n], 16)
                for k in range(KT):
                    m = 4 * n + k
                    if m >= 4:
                        pe.wait_ge(s_wlo, m - 3)
                    for a in range(KT):
                        last = nc.tensor.transpose(PS[m % 4][:, P * a:P * (a + 1)], WS[n % 2][:, a, P * k:P * (k + 1)], ident[:, :])
                    last.then_inc(s_pe, 1)
            pe.wait_ge(s_act, 17)
            mm(PS[6][:, 0:1], ones[:, :], WSUM, start=True, stop=True).then_inc(s_pe, 1)
            pe.wait_ge(s_dve, 2)
            pe.wait_ge(s_wlo, 16)
            for k in range(KT):
                for a in range(KT):
                    last = nc.tensor.transpose(PS[k][:, P * a:P * (a + 1)], WS[0][:, a, P * k:P * (k + 1)], ident[:, :])
                last.then_inc(s_pe, 1)
            pe.wait_ge(s_bv, 1)
            pe.wait_ge(s_dve, 1)
            for k in range(KT):
                for n, w in enumerate((WH["o"], WL["o"])):
                    last = mm(PS[7][:, :], bv_rep[:, P * k:P * (k + 1)], w[:, k, :].bitcast(F32), start=(k == 0 and n == 0),
                              stop=(k == KT - 1 and n == 1))
            last.then_inc(s_pe, 1)
            pe.wait_ge(s_go, 1)

            def products(out, terms):
                for n, (a, b) in enumerate(terms):
                    last = mm(out, a, b, start=(n == 0), stop=(n == len(terms) - 1))
                return last

            def program(seq, i):
                for stage, j, ps, old in steps(seq, i):
                    kind, u = stage[0], stage[1]
                    if old is not None:
                        sig, value = old_bank(*old)
                        pe.wait_ge(sig.sem, value)
                    if kind == "XT":
                        pe.wait_ge(d_xl[u].sem, d_xl[u].nth(j, 1))
                        for k in range(KT):
                            last = nc.tensor.transpose(ps[:, P * k:P * (k + 1)], x_stage(u)[:, P * k:P * (k + 1)], ident[:, :])
                        last.then_inc(t_xt.sem, 1)
                    elif kind == "V":
                        c = slice(P * u, P * (u + 1))
                        if u == 0:
                            pe.wait_ge(v_xlo.sem, v_xlo.nth(j, TT))
                        terms = [t for k in range(KT) for t in (
                            (XH[:, k, c], WH["v"][:, k, :]), (XH[:, k, c], WL["v"][:, k, :]), (XL[:, k, c], WH["v"][:, k, :]))]
                        products(ps[:, :], terms).then_inc(t_v.sem, 1)
                    elif kind == "P":
                        w, g, h, part = "kq"[u // NG], u % NG, stage[2], stage[3]
                        o, c = slice(P * g, P * (g + 1)), slice(HALF * h, HALF * (h + 1))
                        if u == 0 and h == 0 and part == 0:
                            pe.wait_ge(v_xlo.sem, v_xlo.nth(j, TT))
                        terms = [t for k in range(KT) for t in (
                            (WH[w][:, k, o], XH[:, k, c]), (WL[w][:, k, o], XH[:, k, c]), (WH[w][:, k, o], XL[:, k, c]))]
                        for n in range(6 * part, 6 * part + 6):
                            last = mm(ps[:, :], *terms[n], start=(n == 0), stop=(n == len(terms) - 1))
                        if part:
                            last.then_inc(t_p.sem, 1)
                    elif kind == "N":
                        pe.wait_ge(a_p.sem, a_p.nth(j, 4 * u + 4))
                        for c in range(4):
                            last = mm(ps[DH * c:DH * (c + 1), 0:256], NP_[:, :], SQ[:, 256 * c:256 * (c + 1)],
                                      start=True, stop=True, tile_position=(0, DH * c))
                        last.then_inc(t_n.sem, 1)
                    elif kind == "F":
                        r = stage[2]
                        if r == 0:
                            unit_lifted(pe, j, u)
                            norms_lifted(pe, j, u)
                        slot = ST[:, u % 2, :]
                        if u < NG:
                            for p in range(2):
                                a, b = L * p + P * r, L * (2 + p) + P * r
                                last = products(ps[:, 256 * p:256 * (p + 1)], [(slot[:, a:a + P], MA[:, :]),
                                                                              (slot[0:KK, b:b + P], MB[0:KK, p, :])])
                        else:
                            h, half = r % 4, r // 4
                            c = L * h + HALF * half
                            last = mm(ps[:, :], WQS[0:QK, h, :], slot[0:QK, c:c + HALF], start=True, stop=True)
                        last.then_inc(t_f.sem, 1)
                    elif kind == "G":
                        r, kv = stage[2], ND[u % 2]
                        pe.wait_ge(a_exp.sem, a_exp.nth(j, 8 * u + r + 1))
                        if r == 0:
                            if u == 0:
                                pe.wait_ge(a_v.sem, a_v.nth(j, TT))
                            if u < 2:
                                pe.wait_ge(v_a.sem, v_a.nth(j, u - 1))
                            else:
                                pe.wait_ge(a_kc.sem, a_kc.nth(j, 3 * (u - 1)))
                        for h in range(HG):
                            rows = slice(DH * h, DH * (h + 1))
                            last = mm(kv[rows, 0:M + 1], VA[:, r, P * u + DH * h:P * u + DH * (h + 1)], FE[:, r % 4, h, :],
                               start=(r == 0), stop=(r == 7), tile_position=(0, DH * h), skip_group_check=True)
                        if r == 7:
                            pe.wait_ge(v_ks.sem, v_ks.nth(j, 7 * u + 7))
                            for h in range(HG):
                                rows = slice(DH * h, DH * (h + 1))
                                last = mm(kv[rows, 2 * M:3 * M], ones[:, 0:DH], DR[:, u % 2, M * h:M * (h + 1)],
                                          start=False, stop=True, tile_position=(0, DH * h), skip_group_check=True)
                        last.then_inc(t_g.sem, 1)
                    elif kind == "KVT":
                        pe.wait_ge(a_kc.sem, a_kc.nth(j, 3 * u + 3))
                        nc.tensor.transpose(ps[:, 0:P], KVT[:, 0:M], ident[:, :])
                        nc.tensor.transpose(ps[:, P:2 * P], KVT[:, M:2 * M], ident[:, :]).then_inc(t_kvt.sem, 1)
                    elif kind == "GG":
                        g, half = u - NG, stage[2]
                        if half == 0:
                            pe.wait_ge(v_kvc.sem, v_kvc.nth(j, g + 1))
                        if g == 0:
                            pe.wait_ge(a_kc.sem, a_kc.nth(j, 3 * (half + 3)))
                        else:
                            pe.wait_ge(v_a.sem, v_a.nth(j, 2 * (g - 1) + half + 1))
                        pe.wait_ge(a_den.sem, a_den.nth(j, 2 * g + half))
                        pe.wait_ge(a_exp.sem, a_exp.nth(j, 8 * u + 4 * half + 4))
                        for bank, c in ((DN, P), (ND[half], 0)):
                            for h in range(HG):
                                last = mm(bank[DH * h:DH * (h + 1), :], KVS[:, g, c + DH * h:c + DH * (h + 1)],
                                          FE[:, h, :, 0:M], start=True, stop=True, tile_position=(0, DH * h))
                        last.then_inc(t_gg.sem, 1)
                    elif kind == "O":
                        pe.wait_ge(v_alo.sem, v_alo.nth(j, u + 1))
                        ah = ST[:, 1, D * (u % 2):D * (u % 2 + 1)]
                        al = ST[:, 1, 1024 + D * (u % 2):1024 + D * (u % 2 + 1)]
                        terms = [t for k in range(KT) for t in (
                            (ah[:, P * k:P * (k + 1)], WH["o"][:, k, :]), (ah[:, P * k:P * (k + 1)], WL["o"][:, k, :]),
                            (al[:, P * k:P * (k + 1)], WH["o"][:, k, :]))]
                        products(ps[:, :], terms).then_inc(t_o.sem, 1)
                    elif kind == "YT":
                        pe.wait_ge(a_y.sem, a_y.nth(j, u + 1))
                        for k in range(KT):
                            last = nc.tensor.transpose(ps[:, P * k:P * (k + 1)], XR[:, u % 4, P * k:P * (k + 1)], ident[:, :])
                        last.then_inc(t_yt.sem, 1)
                    elif kind == "FF":
                        pe.wait_ge(v_ylo.sem, v_ylo.nth(j, u + 1))
                        terms = [t for k in range(KT) for t in (
                            (ST[:, 1, 2048 + P * k:2048 + P * (k + 1)], WT3[:, k, :]),
                            (ST[:, 1, 2560 + P * k:2560 + P * (k + 1)], WT3[:, k, :]))]
                        products(ps[:, :], terms).then_inc(t_ff.sem, 1)

            batches(pe, program)


_INS = ["L0_attn_x", "L0_attn_Wq", "L0_attn_bq", "L0_attn_Wk", "L0_attn_bk", "L0_attn_Wv", "L0_attn_bv",
        "L0_attn_Wo", "L0_attn_bo", "L0_attn_orf", "L0_ffn_weight"]


def kernel(**inputs):
    import numpy as _np
    import concourse.bacc as _bacc
    from concourse import mybir as _mybir
    from concourse.bass_utils import run_bass_kernel_spmd as _run

    nc = _bacc.Bacc("TRN2", target_bir_lowering=False, num_devices=1)
    arrays, args = {}, []
    for name in _INS:
        a = _np.ascontiguousarray(inputs[name])
        arrays[f"in_{name}"] = a
        args.append(nc.dram_tensor(f"in_{name}", a.shape, _mybir.dt.from_np(a.dtype), kind="ExternalInput").ap())
    args.append(nc.dram_tensor("out_0", (B, L, D), _mybir.dt.float32, kind="ExternalOutput").ap())
    attention_kernel(nc, *args)
    r = _run(nc, [arrays], core_ids=[0])
    return r.results[0]["out_0"]
```

```python
import math
from contextlib import ExitStack

import concourse.bass as bass
from concourse import mybir

F32, F32R = mybir.dt.float32, mybir.dt.float32r
ACT, ALU = mybir.ActivationFunctionType, mybir.AluOpType

B, L, D, H, DH, M = 8, 1024, 512, 16, 32, 128
P = 128
KT = D // P
TT = L // P
HG = 4
NG = H // HG
NU = 2 * NG
HALF = L // 2
EPS, LN_EPS, W_EPS = 1e-6, 1e-5, 1e-5
C_EXP = DH ** -0.25
A_SQ = math.sqrt(1.0 / (2.0 * math.sqrt(DH)) / C_EXP)
NR = 2 * HG
QK = 3 * DH + NR
KK = 2 * DH + NR


def is_key(u):
    return u % 2 == 0


def unit_stages(u, more):
    g = u // 2

    def f(*tiles):
        return [("F", u, n) for n in tiles]

    def also(*stages):
        return list(stages) if more else []

    def xt(*tiles):
        return also(*[("XT", t) for t in tiles])

    if u < NU - 2:
        p = [[("P", u + 2, h, part)] for h in range(2) for part in range(2)]
        s0, s1, l0, l1 = ([(kind, u + 2, h)] for kind in "SL" for h in range(2))
    elif is_key(u):
        p, s0, s1, l0, l1 = [[], [], xt(2), xt(4)], [], [], xt(3), []
    else:
        p = [xt(5), xt(6), also(("P", 0, 0, 0), ("P", 0, 0, 1)), also(("P", 0, 1, 0), ("P", 0, 1, 1))]
        s0, s1, l0, l1 = (also((kind, 0, h)) for kind in "SL" for h in range(2))
    if is_key(u):
        seq = f(0, 1) + p[0] + ([("N", 1)] if u == 0 else []) + p[1] + [("G", g, 0)]
        between = {1: s0, 3: p[2], 6: p[3]}
        for r in range(1, 7):
            seq += (l0 if r == 6 else []) + f(r + 1) + between.get(r, []) + [("G", g, r)]
        return seq + s1 + l1
    seq = f(0, 1) + [("G", g, 7)] + p[0] + ([("N", u + 1)] if u + 1 < NU else []) + f(2, 3) + [("KVT", g)]
    seq += p[1] + ([("R", g - 1, 1, 1)] if u == NU - 1 else [])
    if u < NU - 1:
        seq += s0 + [("GG", g, 0), ("R", g, 0)] + f(4, 5) + p[2] + f(6, 7) + p[3] + l0 + s1 + l1
        return seq + [("GG", g, 1), ("N", u + 2)] + (xt(0, 1) + [("R", g, 1, 0)] if u + 2 == NU - 1 else [("R", g, 1)])
    seq += [("GG", g, 0)] + xt(7) + [("R", g, 0)] + f(4, 5) + p[2] + f(6, 7) + s0 + [("A", 0), ("A", 1)]
    return seq + p[3][:1] + [("GG", g, 1)] + l0 + p[3][1:] + s1 + l1


def output_stages(more):
    def also(*stages):
        return list(stages) if more else []

    seq = [("O", 0), ("LN", 0), ("A", 2), ("R", NG - 1, 1, 0), ("O", 1), ("LN", 1), ("Y", 0), ("A", 3)]
    seq += [("O", 2), ("YT", 0), ("LN", 2), ("Y", 1)] + also(("V", 0)) + [("R", NG - 1, 1, 1), ("FF", 0)]
    seq += also(("N", 0)) + [("YT", 1)]
    for t in range(3, TT):
        seq += ([("A", t + 1)] if t + 1 < TT else []) + [("O", t), ("LN", t), ("Y", t - 1), ("ST", t - 3)]
        seq += [("FF", t - 2)] + also(("V", t - 2)) + [("YT", t - 1)]
    seq += also(("V", TT - 2)) + [("ST", TT - 3), ("FF", TT - 2), ("Y", TT - 1)] + also(("P", 1, 0, 0))
    seq += [("YT", TT - 1)]
    seq += also(("P", 1, 0, 1), ("S", 1, 0), ("L", 1, 0)) + [("FF", TT - 1)]
    seq += also(("V", TT - 1)) + [("ST", TT - 2)]
    return seq + also(("P", 1, 1, 0), ("P", 1, 1, 1), ("S", 1, 1), ("L", 1, 1)) + [("ST", TT - 1)]


def projected(u, h):
    return [("P", u, h, 0), ("P", u, h, 1), ("S", u, h), ("L", u, h)]


PROLOGUE = [("XT", t) for t in range(6)] + [("V", 0), ("XT", 6), ("XT", 7)]
PROLOGUE += projected(0, 0) + projected(0, 1) + [("V", 1), ("N", 0)]
PROLOGUE += [("V", t) for t in range(2, 5)] + projected(1, 0) + [("V", 5)] + projected(1, 1) + [("V", 6), ("V", 7)]
BODY = [s for u in range(NU) for s in unit_stages(u, True)] + output_stages(True)
LAST = [s for u in range(NU) for s in unit_stages(u, False)] + output_stages(False)

RING = {"V": "pj", "P": "pj", "O": "pj", "FF": "pj", "XT": "pj", "F": "ft", "YT": "ft", "N": "nb"}
RING_SIZE = {"pj": 2, "ft": 2, "nb": 1}


def bank_uses(seq, before):
    uses = {ring: list(before[ring]) for ring in RING_SIZE}
    out = []
    for n, stage in enumerate(seq):
        ring = RING.get(stage[0])
        if stage[0] in ("S", "L", "LN"):
            source = ("O", stage[1]) if stage[0] == "LN" else ("P", *stage[1:], 0)
            out.append((next(bank for s, (bank, _) in zip(seq, out) if s == source), None))
            continue
        if ring is None:
            out.append((None, None))
            continue
        size = RING_SIZE[ring]
        mine = uses[ring]
        if stage[0] == "P" and stage[3]:
            out.append((out[mine[-1][0]][0], None))
            continue
        old = mine[-size] if len(mine) >= size else None
        out.append(((len(mine) - len(before[ring])) % size, old))
        mine.append((n, stage))
    return out


def tail(seq):
    out = {}
    for ring, size in RING_SIZE.items():
        mine = [(None, s) for s in seq if RING.get(s[0]) == ring and not (s[0] == "P" and s[3])]
        out[ring] = mine[-size:]
    return out


def attention_kernel(nc, x, Wq, bq, Wk, bk, Wv, bv, Wo, bo, orf, wff, out):
    x_tiles = x.rearrange("b (t p) d -> b t p d", p=P)
    out_tiles = out.rearrange("b (t p) d -> b t p d", p=P)

    ctx = ExitStack()
    with ctx:
        def sb(name, shape, dt=F32):
            return ctx.enter_context(nc.sbuf_tensor(name, shape, dt))

        def sem(name):
            return ctx.enter_context(nc.semaphore(name))

        WH = {w: sb(f"W{w}_hi", [P, KT, D], F32R) for w in "qkvo"}
        WL = {w: sb(f"W{w}_lo", [P, KT, D], F32R) for w in "qkvo"}
        WT3 = sb("W_ternary", [P, KT, D], F32R)
        XH, XL = sb("x_hi", [P, KT, L], F32R), sb("x_lo", [P, KT, L], F32R)
        VA = sb("values_then_attention", [P, TT, D])
        ST = sb("stacks", [P, 2, 4 * L], F32R)
        EH, EL = sb("unit_hi", [P, 2, L], F32R), sb("unit_lo", [P, L], F32R)
        SQ = sb("squares_then_x", [P, L])
        FE = sb("features", [P, 4, HG, M + 1])
        XR = sb("rows", [P, 4, D])
        BO = sb("out_bias", [P, D])
        ident = sb("ident", [P, P])
        WQS = sb("orf_query", [P, HG, M], F32R)
        MA = sb("orf_key_a", [P, 2 * M], F32R)
        MB = sb("orf_key_b", [P, 2, 2 * M], F32R)
        NP_ = sb("norm_columns", [P, DH])
        ones = sb("ones", [P, P])
        KVS = sb("kv_ksum", [P, NG, 2 * P])
        KVT = sb("kv_ksum_t", [P, 2 * P])
        NH, NN = sb("norm_hi", [P, 2 * P], F32R), sb("norm_rows", [P, 2 * P], F32R)
        DR = sb("den", [P, 2, HALF])
        cols = sb("cols", [P, 128])

        def col(a, n=1):
            return cols[:, a:a + n]

        BC, ABC, BVC = col(0, NU), col(NU, NU), col(2 * NU, KT)
        NEGM, EPSL, EXPO, EV = col(20), col(21), col(22), col(23)
        WSUM, SC, HS, NHS = col(24), col(25), col(26), col(27)
        RSUM, CC = col(28, 2 * NG), col(36, 2 * NG)
        stats = sb("stats", [P, 2, 4, 12])

        def ln(kind, t, a, n=1):
            return stats[:, kind, t % 4, a:a + n]

        PS = [ctx.enter_context(nc.psum_tensor(f"ps{i}", [P, 512], F32)) for i in range(8)]
        BANKS = {"pj": PS[0:2], "ft": PS[2:4], "nb": PS[4:5]}
        ND, DN = PS[5:7], PS[7]

        class Signal:

            def __init__(self, name, per, credit=0, step=1):
                self.sem, self.per, self.credit, self.step = sem(name), per, credit, step

            def nth(self, batch, k):
                return batch[0] * (self.per * self.step) + (self.credit + k + batch[1] * self.per) * self.step

        t_xt, t_v, t_p = Signal("xt_done", TT), Signal("v_done", TT), Signal("p_done", 2 * NU)
        t_n, t_kvt = Signal("n_done", NU, 1), Signal("kvt_done", NG, 1)
        t_f, t_g, t_gg = Signal("f_done", 8 * NU, 9), Signal("g_done", 8 * NG), Signal("gg_done", 2 * NG, 1)
        t_o, t_yt, t_ff = Signal("o_done", TT), Signal("yt_done", TT), Signal("ff_done", TT, 1)
        a_xhi, a_v, a_p = Signal("x_hi_ready", TT), Signal("v_ready", TT), Signal("unit_hi_sq_ready", 4 * NU)
        a_exp, a_kc = Signal("features_ready", 8 * NU), Signal("kv_copied", 3 * NG)
        a_den, a_ahi = Signal("den_copied", 2 * NG, 1), Signal("a_hi_ready", TT)
        a_y, a_yhi, a_out = Signal("y_ready", TT), Signal("y_hi_ready", TT), Signal("out_ready", TT)
        v_xlo, v_plo, v_n = Signal("x_lo_ready", TT), Signal("unit_lo_ready", 2 * NU), Signal("norms_ready", 2 * NU)
        v_ks = Signal("features_added", 7 * NG)
        v_kvc, v_c = Signal("kv_ready", NG), Signal("eps_sums_ready", NG)
        v_rc, v_a = Signal("reciprocal_ready", 2 * NG, 0, 2), Signal("attention_ready", 2 * NG, 2, 2)
        v_alo, v_ylo = Signal("a_lo_ready", TT, TT), Signal("y_lo_ready", TT, 2)
        v_ln = [Signal("ln1_steps", 5 * TT, 1), Signal("ln2_steps", 5 * TT, 4)]
        g_xb = Signal("x_plus_bias_ready", TT)
        g_ln = [Signal("ln1_scale_ready", 2 * TT), Signal("ln2_scale_ready", 2 * TT)]
        d_xl = [Signal(f"x_loaded{t}", 1, 0, 16) for t in range(TT)]
        d_xr = [Signal(f"rows_loaded{t}", 1, 0, 16) for t in range(TT)]
        d_st = [Signal(f"rows_stored{s}", TT // 4, 1, 16) for s in range(4)]
        KEY_LIFTS, QUERY_LIFTS = 10, 12
        lifted = [Signal("keys_lifted", NG * KEY_LIFTS, 1, 16), Signal("queries_lifted", NG * QUERY_LIFTS, 1, 16)]
        n_lifted = [Signal("norms_lifted_even", 4 * (NG - 1), 0, 16), Signal("norms_lifted_odd", 4 * NG, 0, 16)]
        n_first = Signal("norms_lifted_first", 4, 0, 16)

        def lifts(u):
            return (KEY_LIFTS if is_key(u) else QUERY_LIFTS) * (u // 2 + 1)

        def unit_lifted(eng, j, u):
            if u < 0:
                eng.wait_ge(lifted[u % 2].sem, lifted[u % 2].nth(j, 0))
            else:
                eng.wait_ge(lifted[u % 2].sem, lifted[u % 2].nth(j, lifts(u)))

        def norms_lifted(eng, j, u):
            if u < 0:
                if j[1]:
                    eng.wait_ge(n_lifted[1].sem, n_lifted[1].nth(j, 0))
            elif u == 0:
                eng.wait_ge(n_first.sem, n_first.nth(j, 4))
            else:
                eng.wait_ge(n_lifted[u % 2].sem, n_lifted[u % 2].nth(j, 4 * ((u + 1) // 2)))

        def lift_norms(queue, wait, sig, j, u):
            slot = ST[:, u % 2, :].bitcast(F32)
            wait(v_n.sem, v_n.nth(j, 2 * u + 2))
            for c in range(4):
                src = NN[DH * c:DH * c + NR, :].bitcast(F32).unsqueeze(1)
                if is_key(u):
                    dst = slot[2 * DH:2 * DH + NR, 2 * L:4 * L].rearrange("p (a t) -> p a t", a=2)
                    n = 2
                else:
                    dst = slot[3 * DH:3 * DH + NR, :].rearrange("p (a t) -> p a t", a=HG)
                    n = HG
                queue.dma_start(dst[:, :, 256 * c:256 * (c + 1)], src.broadcast_to([NR, n, 256])).then_inc(sig.sem, 16)

        s_ld, s_k, s_pe, s_act, s_dve, s_pool = (sem(n) for n in (
            "setup_loaded", "setup_consts", "setup_pe", "setup_act", "setup_dve", "setup_pool"))
        s_wlo, s_chain, s_bv = sem("setup_w_lo"), sem("setup_chain"), sem("setup_bv")
        s_go, s_pin = sem("setup_finished"), sem("carries_a_wait")
        s_ld2 = [sem(f"setup_w{n}") for n in range(5)]

        WS = [VA[:, 4 * n:4 * n + 4, :] for n in range(2)]
        sources = [Wq, Wk, Wv, Wo, wff]
        orf_rep = DR[:, 1, 0:P]
        bv_rep = DR[:, 0, :]
        lo_rows = FE[:, 1, 0, 0:4 * HG]

        def x_stage(t):
            return XR[:, t, :] if t < 4 else SQ[:, D * (t % 2):D * (t % 2 + 1)]

        def x_rows(t):
            return XR[:, t, :].rearrange("p (a m) -> p a m", a=HG) if t < 4 else FE[:, t - 4, :, 0:M]

        def old_bank(stage, j):
            kind, k = stage[0], stage[1]
            if kind == "V":
                return a_v, a_v.nth(j, k + 1)
            if kind == "P":
                return v_plo, v_plo.nth(j, 2 * k + stage[2] + 1)
            if kind == "O":
                return v_ln[0], v_ln[0].nth(j, 5 * k + 1)
            if kind == "FF":
                return v_ln[1], v_ln[1].nth(j, 5 * k + 1)
            if kind == "F":
                return a_exp, a_exp.nth(j, 8 * k + stage[2] + 1)
            if kind == "XT":
                return v_xlo, v_xlo.nth(j, k + 1)
            if kind == "YT":
                return v_ylo, v_ylo.nth(j, k + 1)
            return v_n, v_n.nth(j, 2 * k + 2)

        def looks_ahead(stage):
            return stage[0] in ("XT", "V") or stage[:2] == ("N", 0) or (stage[0] in "PSL" and stage[1] < 2)

        none = {ring: [] for ring in RING_SIZE}
        BANKING = {id(PROLOGUE): bank_uses(PROLOGUE, none), id(BODY): bank_uses(BODY, tail(BODY)),
                   id(LAST): bank_uses(LAST, tail(BODY))}

        def steps(seq, j):
            for n, (stage, (bank, old)) in enumerate(zip(seq, BANKING[id(seq)])):
                mine = (j, 1) if seq is BODY and looks_ahead(stage) else (j, 0)
                if old is not None:
                    m, prev = old
                    if m is None:
                        old = (prev, (j, 0 if looks_ahead(prev) else -1))
                    else:
                        old = (prev, (j, 1 if seq is BODY and looks_ahead(prev) else 0))
                yield stage, mine, (None if bank is None else BANKS[RING.get(stage[0], "pj")][bank]), old

        def batches(eng, program):
            program(PROLOGUE, 0)
            with eng.Fori(0, B - 1) as i:
                program(BODY, i)
            program(LAST, B - 1)

        block = ctx.enter_context(nc.Block())

        @block.sync
        def _(sp):
            sp.dma_start(BC[:, 0::2], bk.rearrange("(g p) -> p g", p=P), allow_slow_non_contiguous=True).then_inc(s_ld, 16)
            sp.dma_start(BC[:, 1::2], bq.rearrange("(g p) -> p g", p=P), allow_slow_non_contiguous=True).then_inc(s_ld, 16)
            sp.dma_start(BVC, bv.rearrange("(g p) -> p g", p=P), allow_slow_non_contiguous=True).then_inc(s_ld, 16)
            sp.dma_start(BO[:, :], bo.unsqueeze(0).broadcast_to([P, D])).then_inc(s_ld, 16)
            for r in range(4):
                sp.dma_start(orf_rep[:, DH * r:DH * (r + 1)], orf).then_inc(s_ld, 16)
            for n, w in enumerate(sources):
                if n >= 2:
                    sp.wait_ge(s_pe, 4 * (n - 1) + 1)
                sp.dma_start(WS[n % 2], w.rearrange("(a p) i -> p a i", p=P)).then_inc(s_ld2[n], 16)
            for sig in lifted:
                sp.sem_inc(sig.sem, sig.credit * sig.step)

            def wait(semaphore, value):
                sp.wait_ge(semaphore, value)
                sp.sem_inc(s_pin, 1)

            def load_x(j, t):
                sp.dma_start(x_stage(t), x_tiles[j[0] + j[1], t]).then_inc(d_xl[t].sem, 16)

            def load_rows(j, t, ahead=False):
                if t == 0 and ahead:
                    wait(t_xt.sem, t_xt.nth((j[0], 1), 4))
                elif t < 4 and not ahead:
                    wait(d_st[t].sem, d_st[t].nth(j, 0))
                elif t == 4:
                    wait(t_gg.sem, t_gg.nth(j, 2 * NG))
                sp.dma_start(x_rows(t), x_tiles[j[0] + j[1], t].rearrange("p (a m) -> p a m", a=HG))\
                    .then_inc(d_xr[t].sem, 16)

            def program(seq, i):
                if seq is PROLOGUE:
                    for t in range(4):
                        load_x((0, 0), t)
                for stage, j, _, _ in steps(seq, i):
                    kind, u = stage[0], stage[1]
                    if kind == "O" and u == 0:
                        for t in range(4, TT):
                            load_rows(j, t)
                    elif kind == "L" and stage[2] == 1:
                        slot = ST[:, u % 2, :].bitcast(F32)
                        hi, lo, sig = EH[:, u % 2, :].bitcast(F32), EL[:, :].bitcast(F32), lifted[u % 2]
                        wait(t_f.sem, t_f.nth(j, 8 * (u - 1)))
                        if u == 1:
                            wait(t_ff.sem, t_ff.nth(j, 0))
                        wait(a_p.sem, a_p.nth(j, 4 * u + 3))
                        for h in range(HG):
                            src = hi[DH * h:DH * (h + 1), :]
                            if is_key(u):
                                r, c = 2 * DH * (h % 2), L * (h // 2)
                                sp.dma_start(slot[r:r + DH, c:c + L], src).then_inc(sig.sem, 16)
                            else:
                                sp.dma_start(slot[0:DH, L * h:L * (h + 1)], src).then_inc(sig.sem, 16)
                                sp.dma_start(slot[2 * DH:3 * DH, L * h:L * (h + 1)], src).then_inc(sig.sem, 16)
                        if is_key(u):
                            for p in range(2):
                                sp.dma_start(slot[0:2 * DH, L * (2 + p):L * (3 + p)],
                                             hi[2 * DH * p:2 * DH * (p + 1), :]).then_inc(sig.sem, 16)
                        wait(v_plo.sem, v_plo.nth(j, 2 * u + 2))
                        for h in range(HG):
                            r, c = (2 * DH * (h % 2) + DH, L * (h // 2)) if is_key(u) else (DH, L * h)
                            sp.dma_start(slot[r:r + DH, c:c + L], lo[DH * h:DH * (h + 1), :]).then_inc(sig.sem, 16)
                    elif kind == "N" and u == 0:
                        lift_norms(sp, wait, n_first, j, 0)
                    elif kind == "N" and u == NU - 2 and seq is BODY:
                        for t in range(4):
                            wait(d_st[t].sem, d_st[t].nth(j, 0))
                            load_x((i, 1), t)
                    elif kind == "XT" and u == 4 and seq is BODY or kind == "N" and u == NU - 1 and seq is LAST:
                        for t in range(4):
                            load_rows((i, 0), t, seq is BODY)

            batches(sp, program)

        @block.gpsimd
        def _(pool):
            filled = [1]

            def fill_where(t, base, pattern, cm, fill):
                pool.wait_ge(s_k, filled[0])
                filled[0] += 1
                nc.gpsimd.affine_select(out=t, in_=t, compare_op=ALU.not_equal, fill=fill, base=base,
                                        pattern=pattern, channel_multiplier=cm).then_inc(s_k, 1)

            nc.gpsimd.memset(ident[:, :], 0.0)
            nc.gpsimd.memset(ones[:, :], 1.0)
            nc.gpsimd.memset(NP_[:, :], 0.0)
            nc.gpsimd.memset(lo_rows, 0.0)
            nc.gpsimd.memset(FE[:, 2, :, :], 0.0)
            nc.gpsimd.memset(EXPO, -0.5)
            nc.gpsimd.memset(EPSL, EPS * L)
            for t in (WQS, MA, MB):
                last = nc.gpsimd.memset(t[:].bitcast(F32), 0.0)
            last.then_inc(s_k, 1)
            fill_where(ident[:, :], 0, [[-1, P]], 1, 1.0)
            pool.wait_ge(s_k, filled[0])
            filled[0] += 1
            for h in range(HG):
                nc.gpsimd.memset(NP_[DH * h:DH * (h + 1), h:h + 1], 1.0)
                last = nc.gpsimd.memset(NP_[DH * h:DH * (h + 1), HG + h:HG + h + 1], 1.0)
            last.then_inc(s_k, 1)
            fill_where(lo_rows.rearrange("p (a b) -> p a b", a=4), -HG, [[-DH, 4], [-1, HG]], 1, -1.0)
            q_rows = FE[3 * DH:QK, 2, :, 0:M]
            fill_where(q_rows, 0, [[-1, HG], [0, M]], 1, -1.0)
            fill_where(q_rows, -HG, [[-1, HG], [0, M]], 1, -1.0)
            k_rows = FE[2 * DH:KK, 2, :, 0:M]
            fill_where(k_rows, 0, [[-1, HG], [0, M]], 1, -1.0)
            fill_where(k_rows, -HG, [[-1, HG], [0, M]], 1, -1.0)
            pool.wait_ge(s_k, filled[0])
            pool.wait_ge(s_dve, 1)
            pool.wait_ge(s_pe, 1)
            nc.gpsimd.memset(FE[:, :, :, M:M + 1], 1.0).then_inc(s_pool, 1)

            def layer_scale(k, j, t):
                pool.wait_ge(v_ln[k].sem, v_ln[k].nth(j, 5 * t + 5))
                nc.gpsimd.tensor_tensor(ln(k, t, 10), ln(k, t, 8), EXPO, ALU.pow).then_inc(g_ln[k].sem, 1)
                pool.wait_ge(g_ln[k].sem, g_ln[k].nth(j, 2 * t + 1))
                nc.gpsimd.tensor_tensor(ln(k, t, 11), ln(k, t, 9), ln(k, t, 10), ALU.mult).then_inc(g_ln[k].sem, 1)

            def wait(semaphore, value):
                pool.wait_ge(semaphore, value)
                pool.sem_inc(s_pin, 1)

            def load_x(j, t):
                pool.dma_start(x_stage(t), x_tiles[j[0] + j[1], t]).then_inc(d_xl[t].sem, 16)

            def program(seq, i):
                if seq is PROLOGUE:
                    load_x((0, 0), 4)
                    load_x((0, 0), 5)
                for stage, j, _, _ in steps(seq, i):
                    kind, t = stage[0], stage[1]
                    if kind == "XT" and 4 <= t < 6:
                        wait(t_xt.sem, t_xt.nth(j, t + 1))
                        load_x(j, t + 2)
                    elif kind == "N" and t > 0:
                        if t == NU - 1 and seq is BODY:
                            wait(t_n.sem, t_n.nth(j, NU))
                            load_x((i, 1), 4)
                            load_x((i, 1), 5)
                        lift_norms(pool, wait, n_lifted[t % 2], j, t)
                    elif kind == "A":
                        pool.wait_ge(d_xr[t].sem, d_xr[t].nth(j, 1))
                        nc.gpsimd.tensor_tensor(x_rows(t), x_rows(t), BO[:, :].rearrange("p (a m) -> p a m", a=HG), ALU.add).then_inc(g_xb.sem, 1)
                    elif kind == "LN":
                        layer_scale(0, j, t)
                    elif kind == "FF":
                        layer_scale(1, j, t)
                if seq is PROLOGUE:
                    pool.wait_ge(s_dve, 4)

            batches(pool, program)

        @block.scalar
        def _(act):
            for sig in (a_den,):
                act.sem_inc(sig.sem, sig.credit)
            for sig in d_st:
                act.sem_inc(sig.sem, sig.credit * sig.step)
            for n in range(4):
                w = "qkvo"[n]
                for k in range(KT):
                    act.wait_ge(s_pe, 4 * n + k + 2)
                    nc.scalar.activation(WH[w][:, k, :], PS[(4 * n + k) % 4][:, :], ACT.Copy).then_inc(s_act, 1)
            act.wait_ge(s_ld2[4], 16)
            nc.scalar.activation(WS[1].rearrange("p a i -> p (a i)"), WS[0].rearrange("p a i -> p (a i)"), ACT.Abs,
                                 accum_out=WSUM).then_inc(s_act, 1)
            act.wait_ge(s_go, 1)

            def program(seq, i):
                for stage, j, ps, _ in steps(seq, i):
                    kind, u = stage[0], stage[1]
                    if kind == "XT":
                        act.wait_ge(t_xt.sem, t_xt.nth(j, u + 1))
                        nc.scalar.activation(XH[:, :, P * u:P * (u + 1)], ps[:, :].rearrange("p (k c) -> p k c", k=KT),
                                             ACT.Copy).then_inc(a_xhi.sem, 1)
                    elif kind == "V":
                        act.wait_ge(t_v.sem, t_v.nth(j, u + 1))
                        act.wait_ge(v_alo.sem, v_alo.nth(j, u + 1 - TT))
                        nc.scalar.activation(VA[:, u, :], ps[:, :], ACT.Copy).then_inc(a_v.sem, 1)
                    elif kind == "S":
                        h, half = stage[2], slice(HALF * stage[2], HALF * (stage[2] + 1))
                        act.wait_ge(t_p.sem, t_p.nth(j, 2 * u + h + 1))
                        if h == 0:
                            unit_lifted(act, j, u - 2)
                        nc.scalar.activation(EH[:, u % 2, half], ps[:, :], ACT.Identity, bias=BC[:, u:u + 1]).then_inc(a_p.sem, 1)
                        if h == 0:
                            act.wait_ge(t_n.sem, t_n.nth(j, u))
                        nc.scalar.activation(SQ[:, half], ps[:, :], ACT.Square, bias=ABC[:, u:u + 1],
                                             scale=A_SQ).then_inc(a_p.sem, 1)
                    elif kind == "F":
                        n = 8 * u + stage[2]
                        act.wait_ge(t_f.sem, t_f.nth(j, n + 1))
                        if n == 0:
                            act.wait_ge(v_ln[0].sem, v_ln[0].nth(j, 0))
                        v, r = (n - 4) // 8, (n - 4) % 8
                        if n < 4:
                            act.wait_ge(t_gg.sem, t_gg.nth(j, 0))
                        elif is_key(v):
                            act.wait_ge(t_g.sem, t_g.nth(j, 4 * v + r + 1))
                            act.wait_ge(v_ks.sem, v_ks.nth(j, 7 * (v // 2) + max(r, 1)))
                        else:
                            act.wait_ge(t_gg.sem, t_gg.nth(j, v - 1 + r // 4 + 1))
                        nc.scalar.activation(FE[:, n % 4, :, 0:M], ps[:, :].rearrange("p (a m) -> p a m", a=HG),
                                             ACT.Exp, scale=C_EXP).then_inc(a_exp.sem, 1)
                    elif kind == "G" and stage[2] == 7:
                        kv = ND[0]
                        act.wait_ge(t_g.sem, t_g.nth(j, 8 * u + 8))
                        nc.scalar.activation(EV, kv[:, M:M + 1], ACT.Copy, scale=EPS).then_inc(a_kc.sem, 1)
                        act.wait_ge(t_kvt.sem, t_kvt.nth(j, u))
                        act.wait_ge(a_kc.sem, a_kc.nth(j, 3 * u + 1))
                        nc.scalar.activation(KVT[:, 0:M], kv[:, 0:M], ACT.Identity, bias=EV,
                                             accum_out=RSUM[:, 2 * u:2 * u + 1]).then_inc(a_kc.sem, 1)
                        nc.scalar.activation(KVT[:, M:2 * M], kv[:, 2 * M:3 * M], ACT.Identity, bias=EPSL,
                                             accum_out=RSUM[:, 2 * u + 1:2 * u + 2]).then_inc(a_kc.sem, 1)
                    elif kind == "GG":
                        g, h = u, stage[2]
                        act.wait_ge(t_gg.sem, t_gg.nth(j, 2 * g + h + 1))
                        if h == 0:
                            act.wait_ge(v_c.sem, v_c.nth(j, g + 1))
                        act.wait_ge(v_a.sem, v_a.nth(j, 2 * g + h - 1))
                        nc.scalar.activation(DR[:, h, :], DN[:, :], ACT.Identity,
                                             bias=CC[:, 2 * g + 1:2 * g + 2]).then_inc(a_den.sem, 1)
                    elif kind == "A":
                        split_hi(j, u)
                    elif kind == "Y":
                        apply_norm(0, j, u)
                    elif kind == "YT":
                        act.wait_ge(t_yt.sem, t_yt.nth(j, u + 1))
                        nc.scalar.activation(ST[:, 1, 2048:2560], ps[:, :], ACT.Copy).then_inc(a_yhi.sem, 1)
                    elif kind == "ST":
                        apply_norm(1, j, u)
                        act.wait_ge(a_out.sem, a_out.nth(j, u + 1))
                        act.dma_start(out_tiles[j[0] + j[1], u], XR[:, u % 4, :]).then_inc(d_st[u % 4].sem, 16)

            def split_hi(j, t):
                act.wait_ge(v_a.sem, v_a.nth(j, 7 if t < 4 else 8))
                if t < 2:
                    act.wait_ge(t_f.sem, t_f.nth(j, 8 * NU))
                else:
                    act.wait_ge(t_o.sem, t_o.nth(j, t - 1))
                nc.scalar.activation(ST[:, 1, D * (t % 2):D * (t % 2 + 1)], VA[:, t, :], ACT.Copy).then_inc(a_ahi.sem, 1)

            def apply_norm(k, j, t):
                act.wait_ge(g_ln[k].sem, g_ln[k].nth(j, 2 * t + 2))
                row = XR[:, t % 4, :]
                nc.scalar.activation(row, row, ACT.Identity, scale=ln(k, t, 10), bias=ln(k, t, 11))\
                    .then_inc((a_y, a_out)[k].sem, 1)

            batches(act, program)
            for sig in d_st:
                act.wait_ge(sig.sem, sig.nth((B, 0), 0))

        @block.vector
        def _(dve):
            for sig in (v_a, v_alo, v_ylo, v_ln[0], v_ln[1]):
                dve.sem_inc(sig.sem, sig.credit * sig.step)
            chain = [0]

            def link(ins):
                chain[0] += 1
                ins.then_inc(s_chain, 1)
                dve.wait_ge(s_chain, chain[0])

            dve.wait_ge(s_k, 8)
            nc.vector.reduce_sum(NEGM, lo_rows, axis=mybir.AxisListType.X)
            dve.wait_ge(s_ld, 16 * 8)
            nc.vector.tensor_scalar(ABC, BC, A_SQ, None, ALU.mult)
            for k in range(KT):
                last = nc.vector.tensor_scalar(bv_rep[:, P * k:P * (k + 1)], ones[:, :], BVC[:, k:k + 1], None, ALU.mult)
            last.then_inc(s_bv, 1)
            dve.wait_ge(s_pe, 1)
            wT = PS[7]
            for r in range(2):
                for h in range(HG):
                    nc.vector.tensor_copy(WQS[DH * r:DH * (r + 1), h, :], wT[DH * r:DH * (r + 1), 0:M])
            for r in range(4):
                a = r // 2
                nc.vector.tensor_copy(MA[DH * r:DH * (r + 1), M * a:M * (a + 1)], wT[DH * r:DH * (r + 1), 0:M])
            link(nc.vector.tensor_copy(EH[:, 0, 0:M], wT[:, 0:M]))
            for h in range(HG):
                r = slice(2 * DH, 3 * DH)
                nc.vector.tensor_tensor(WQS[r, h, :], wT[r, 0:M], EH[r, 0, 0:M].bitcast(F32), ALU.subtract)
            for p in range(2):
                for a in range(2):
                    r = slice(DH * a, DH * (a + 1))
                    nc.vector.tensor_tensor(MB[r, p, M * a:M * (a + 1)], wT[r, 0:M], EH[r, 0, 0:M].bitcast(F32), ALU.subtract)
            nc.vector.tensor_copy(WQS[3 * DH:QK, :, :], FE[3 * DH:QK, 2, :, 0:M])
            last = nc.vector.tensor_copy(MB[2 * DH:KK, :, :].rearrange("p a (b m) -> p (a b) m", b=2),
                                         FE[2 * DH:KK, 2, :, 0:M])
            last.then_inc(s_dve, 1)
            for n in range(4):
                w = "qkvo"[n]
                for k in range(KT):
                    dve.wait_ge(s_act, 4 * n + k + 1)
                    nc.vector.tensor_tensor(WL[w][:, k, :], PS[(4 * n + k) % 4][:, :], WH[w][:, k, :].bitcast(F32),
                                            ALU.subtract).then_inc(s_wlo, 1)
            dve.wait_ge(s_pe, 4 * 4 + 2)
            link(nc.vector.tensor_scalar(SC, PS[6][:, 0:1], 1.0 / (D * D), W_EPS, ALU.mult, ALU.max))
            link(nc.vector.tensor_scalar(HS, SC, 0.5, None, ALU.mult))
            link(nc.vector.tensor_scalar(NHS, SC, -0.5, None, ALU.mult))
            wf = WS[0].rearrange("p a i -> p (a i)")
            below = WS[1].rearrange("p a i -> p (a i)")
            link(nc.vector.tensor_scalar(below, wf, NHS, None, ALU.is_lt))
            nc.vector.scalar_tensor_tensor(out=wf, in0=wf, scalar=HS, in1=below, op0=ALU.is_gt,
                                           op1=ALU.subtract).then_inc(s_dve, 1)
            dve.wait_ge(s_pool, 1)
            dve.wait_ge(s_dve, 2)
            dve.sem_inc(s_go, 1)
            for k in range(KT):
                dve.wait_ge(s_pe, 4 * 4 + 4 + k)
                last = nc.vector.tensor_copy(WT3[:, k, :], PS[2 + k][:, :])
            last.then_inc(s_dve, 1)
            nc.vector.tensor_tensor(BO[:, :], PS[7][:, :], BO[:, :], ALU.add).then_inc(s_dve, 1)

            def layer_stats(k, j, t, source):
                sig, row, n = v_ln[k], XR[:, t % 4, :], 5 * t
                source().then_inc(sig.sem, 1)
                dve.wait_ge(sig.sem, sig.nth(j, n + 1))
                nc.vector.bn_stats(ln(k, t, 0, 6), row).then_inc(sig.sem, 1)
                dve.wait_ge(sig.sem, sig.nth(j, n + 2))
                dve.sem_inc(s_pin, 1)
                nc.vector.bn_aggr(ln(k, t, 6, 2), ln(k, t, 0, 6)).then_inc(sig.sem, 1)
                dve.wait_ge(sig.sem, sig.nth(j, n + 3))
                nc.vector.tensor_scalar(ln(k, t, 8), ln(k, t, 7), LN_EPS, None, ALU.add).then_inc(sig.sem, 1)
                nc.vector.tensor_scalar(ln(k, t, 9), ln(k, t, 6), -1.0, None, ALU.mult).then_inc(sig.sem, 1)

            def add_features(j, g, r):
                if r == 0:
                    return
                dve.wait_ge(a_exp.sem, a_exp.nth(j, 16 * g + r + 1))
                total = DR[:, 0, :].rearrange("p (a m) -> p a m", a=HG)
                if r == 1:
                    dve.wait_ge(v_a.sem, v_a.nth(j, max(2 * g - 1, 0)))
                    ins = nc.vector.tensor_tensor(total, FE[:, 0, :, 0:M], FE[:, 1, :, 0:M], ALU.add)
                else:
                    dve.wait_ge(v_ks.sem, v_ks.nth(j, 7 * g + r - 1))
                    ins = nc.vector.tensor_tensor(total, total, FE[:, r % 4, :, 0:M], ALU.add)
                ins.then_inc(v_ks.sem, 1)

            def split_lo(j, t):
                dve.wait_ge(a_ahi.sem, a_ahi.nth(j, t + 1))
                nc.vector.tensor_tensor(ST[:, 1, 1024 + D * (t % 2):1024 + D * (t % 2 + 1)], VA[:, t, :],
                                        ST[:, 1, D * (t % 2):D * (t % 2 + 1)].bitcast(F32), ALU.subtract).then_inc(v_alo.sem, 1)

            def program(seq, i):
                for stage, j, ps, _ in steps(seq, i):
                    kind, u = stage[0], stage[1]
                    if kind == "XT":
                        dve.wait_ge(a_xhi.sem, a_xhi.nth(j, u + 1))
                        c = slice(P * u, P * (u + 1))
                        nc.vector.tensor_tensor(XL[:, :, c], ps[:, :].rearrange("p (k c) -> p k c", k=KT),
                                                XH[:, :, c].bitcast(F32), ALU.subtract).then_inc(v_xlo.sem, 1)
                    elif kind == "L":
                        h, half = stage[2], slice(HALF * stage[2], HALF * (stage[2] + 1))
                        dve.wait_ge(a_p.sem, a_p.nth(j, 2 * (2 * u + h) + 2))
                        if h == 0:
                            unit_lifted(dve, j, u - 1)
                        nc.vector.scalar_tensor_tensor(out=EL[:, half], in0=ps[:, :], scalar=BC[:, u:u + 1],
                                                       in1=EH[:, u % 2, half].bitcast(F32), op0=ALU.add,
                                                       op1=ALU.subtract).then_inc(v_plo.sem, 1)
                    elif kind == "N":
                        dve.wait_ge(t_n.sem, t_n.nth(j, u + 1))
                        norms_lifted(dve, j, u - 1)
                        nc.vector.tensor_copy(NH[:, :], ps[:, 0:256]).then_inc(v_n.sem, 1)
                        dve.wait_ge(v_n.sem, v_n.nth(j, 2 * u + 1))
                        nc.vector.scalar_tensor_tensor(out=NN[:, :], in0=NH[:, :].bitcast(F32), scalar=NEGM,
                                                       in1=ps[:, 0:256], op0=ALU.mult, op1=ALU.add).then_inc(v_n.sem, 1)
                    elif kind == "KVT":
                        dve.wait_ge(t_kvt.sem, t_kvt.nth(j, u + 1))
                        nc.vector.tensor_copy(KVS[:, u, :], DN[:, 0:2 * P]).then_inc(v_kvc.sem, 1)
                    elif kind == "F" and is_key(u):
                        add_features(j, u // 2, stage[2])
                    elif kind == "G" and stage[2] == 7:
                        dve.wait_ge(a_kc.sem, a_kc.nth(j, 3 * u + 3))
                        nc.vector.tensor_scalar(CC[:, 2 * u:2 * u + 2], RSUM[:, 2 * u:2 * u + 2], EPS, None,
                                                ALU.mult).then_inc(v_c.sem, 1)
                    elif kind == "R":
                        g, h = u, stage[2]
                        dve.wait_ge(a_den.sem, a_den.nth(j, 2 * g + h + 1))
                        parts = [stage[3]] if len(stage) > 3 else [0, 1]
                        t0, t1 = 2 * parts[0], 2 * parts[-1] + 2
                        den = DR[:, h, P * t0:P * t1]
                        nc.vector.reciprocal(den, den).then_inc(v_rc.sem, len(parts))
                        dve.wait_ge(v_rc.sem, v_rc.nth(j, 2 * g + h) + parts[-1] + 1)
                        nc.vector.scalar_tensor_tensor(
                            out=VA[:, 4 * h + t0:4 * h + t1, P * g:P * (g + 1)],
                            in0=ND[h][:, P * t0:P * t1].rearrange("p (t c) -> p t c", c=P),
                            scalar=CC[:, 2 * g:2 * g + 1], in1=den.rearrange("p (t c) -> p t c", c=P),
                            op0=ALU.add, op1=ALU.mult).then_inc(v_a.sem, len(parts))
                    elif kind == "A":
                        split_lo(j, u)
                    elif kind == "LN":
                        dve.wait_ge(t_o.sem, t_o.nth(j, u + 1))
                        dve.wait_ge(g_xb.sem, g_xb.nth(j, u + 1))
                        if u >= 4:
                            dve.wait_ge(d_st[u % 4].sem, d_st[u % 4].nth(j, 1))
                        layer_stats(0, j, u, lambda: nc.vector.tensor_tensor(
                            XR[:, u % 4, :].rearrange("p (a m) -> p a m", a=HG), ps[:, :].rearrange("p (a m) -> p a m", a=HG),
                            x_rows(u), ALU.add))
                    elif kind == "YT":
                        dve.wait_ge(a_yhi.sem, a_yhi.nth(j, u + 1))
                        nc.vector.tensor_tensor(ST[:, 1, 2560:3072], ps[:, :], ST[:, 1, 2048:2560].bitcast(F32),
                                                ALU.subtract).then_inc(v_ylo.sem, 1)
                    elif kind == "FF":
                        dve.wait_ge(t_ff.sem, t_ff.nth(j, u + 1))
                        row = XR[:, u % 4, :]
                        layer_stats(1, j, u, lambda: nc.vector.scalar_tensor_tensor(
                            out=row, in0=ps[:, :], scalar=SC, in1=row, op0=ALU.mult, op1=ALU.add))

            batches(dve, program)

        @block.tensor
        def _(pe):
            for sig in (t_n, t_kvt, t_f, t_gg, t_ff):
                pe.sem_inc(sig.sem, sig.credit)
            mm = nc.tensor.matmul
            pe.wait_ge(s_k, 8)
            pe.wait_ge(s_ld, 16 * 8)
            nc.tensor.transpose(PS[7][:, 0:M], orf_rep, ident[:, :]).then_inc(s_pe, 1)
            for n in range(4):
                pe.wait_ge(s_ld2[n], 16)
                for k in range(KT):
                    m = 4 * n + k
                    if m >= 4:
                        pe.wait_ge(s_wlo, m - 3)
                    for a in range(KT):
                        last = nc.tensor.transpose(PS[m % 4][:, P * a:P * (a + 1)], WS[n % 2][:, a, P * k:P * (k + 1)], ident[:, :])
                    last.then_inc(s_pe, 1)
            pe.wait_ge(s_act, 17)
            mm(PS[6][:, 0:1], ones[:, :], WSUM, start=True, stop=True).then_inc(s_pe, 1)
            pe.wait_ge(s_bv, 1)
            pe.wait_ge(s_dve, 1)
            pe.wait_ge(s_wlo, 16)
            for k in range(KT):
                for n, w in enumerate((WH["o"], WL["o"])):
                    last = mm(PS[7][:, :], bv_rep[:, P * k:P * (k + 1)], w[:, k, :].bitcast(F32), start=(k == 0 and n == 0),
                              stop=(k == KT - 1 and n == 1))
            last.then_inc(s_pe, 1)
            pe.wait_ge(s_dve, 2)
            for k in range(KT):
                for a in range(KT):
                    last = nc.tensor.transpose(PS[2 + k][:, P * a:P * (a + 1)], WS[0][:, a, P * k:P * (k + 1)], ident[:, :])
                last.then_inc(s_pe, 1)
            pe.wait_ge(s_go, 1)

            def products(out, terms):
                for n, (a, b) in enumerate(terms):
                    last = mm(out, a, b, start=(n == 0), stop=(n == len(terms) - 1))
                return last

            def program(seq, i):
                for stage, j, ps, old in steps(seq, i):
                    kind, u = stage[0], stage[1]
                    if old is not None:
                        sig, value = old_bank(*old)
                        pe.wait_ge(sig.sem, value)
                    if kind == "XT":
                        pe.wait_ge(d_xl[u].sem, d_xl[u].nth(j, 1))
                        for k in range(KT):
                            last = nc.tensor.transpose(ps[:, P * k:P * (k + 1)], x_stage(u)[:, P * k:P * (k + 1)], ident[:, :])
                        last.then_inc(t_xt.sem, 1)
                    elif kind == "V":
                        c = slice(P * u, P * (u + 1))
                        pe.wait_ge(v_xlo.sem, v_xlo.nth(j, u + 1))
                        terms = [t for k in range(KT) for t in (
                            (XH[:, k, c], WH["v"][:, k, :]), (XH[:, k, c], WL["v"][:, k, :]), (XL[:, k, c], WH["v"][:, k, :]))]
                        products(ps[:, :], terms).then_inc(t_v.sem, 1)
                    elif kind == "P":
                        w, g, h, part = "kq"[u % 2], u // 2, stage[2], stage[3]
                        o, c = slice(P * g, P * (g + 1)), slice(HALF * h, HALF * (h + 1))
                        if u == 0 and h == 0 and part == 0:
                            pe.wait_ge(v_xlo.sem, v_xlo.nth(j, TT))
                        terms = [t for k in range(KT) for t in (
                            (WH[w][:, k, o], XH[:, k, c]), (WL[w][:, k, o], XH[:, k, c]), (WH[w][:, k, o], XL[:, k, c]))]
                        for n in range(6 * part, 6 * part + 6):
                            last = mm(ps[:, :], *terms[n], start=(n == 0), stop=(n == len(terms) - 1))
                        if part:
                            last.then_inc(t_p.sem, 1)
                    elif kind == "N":
                        pe.wait_ge(a_p.sem, a_p.nth(j, 4 * u + 4))
                        for c in range(4):
                            last = mm(ps[DH * c:DH * (c + 1), 0:256], NP_[:, :], SQ[:, 256 * c:256 * (c + 1)],
                                      start=True, stop=True, tile_position=(0, DH * c))
                        last.then_inc(t_n.sem, 1)
                    elif kind == "F":
                        r = stage[2]
                        if r == 0:
                            unit_lifted(pe, j, u)
                            norms_lifted(pe, j, u)
                        slot = ST[:, u % 2, :]
                        if is_key(u):
                            for p in range(2):
                                a, b = L * p + P * r, L * (2 + p) + P * r
                                last = products(ps[:, 256 * p:256 * (p + 1)], [(slot[:, a:a + P], MA[:, :]),
                                                                              (slot[0:KK, b:b + P], MB[0:KK, p, :])])
                        else:
                            h, half = r % 4, r // 4
                            c = L * h + HALF * half
                            last = mm(ps[:, :], WQS[0:QK, h, :], slot[0:QK, c:c + HALF], start=True, stop=True)
                        last.then_inc(t_f.sem, 1)
                    elif kind == "G":
                        r, kv = stage[2], ND[0]
                        pe.wait_ge(a_exp.sem, a_exp.nth(j, 16 * u + r + 1))
                        if r == 0:
                            if u == 0:
                                pe.wait_ge(a_v.sem, a_v.nth(j, TT))
                            pe.wait_ge(v_a.sem, v_a.nth(j, max(2 * u - 1, 0)))
                        for h in range(HG):
                            rows = slice(DH * h, DH * (h + 1))
                            last = mm(kv[rows, 0:M + 1], VA[:, r, P * u + DH * h:P * u + DH * (h + 1)], FE[:, r % 4, h, :],
                               start=(r == 0), stop=(r == 7), tile_position=(0, DH * h), skip_group_check=True)
                        if r == 7:
                            pe.wait_ge(v_ks.sem, v_ks.nth(j, 7 * u + 7))
                            for h in range(HG):
                                rows = slice(DH * h, DH * (h + 1))
                                last = mm(kv[rows, 2 * M:3 * M], ones[:, 0:DH], DR[:, 0, M * h:M * (h + 1)],
                                          start=False, stop=True, tile_position=(0, DH * h), skip_group_check=True)
                        last.then_inc(t_g.sem, 1)
                    elif kind == "KVT":
                        pe.wait_ge(a_kc.sem, a_kc.nth(j, 3 * u + 3))
                        pe.wait_ge(a_den.sem, a_den.nth(j, 2 * u))
                        nc.tensor.transpose(DN[:, 0:P], KVT[:, 0:M], ident[:, :])
                        nc.tensor.transpose(DN[:, P:2 * P], KVT[:, M:2 * M], ident[:, :]).then_inc(t_kvt.sem, 1)
                    elif kind == "GG":
                        g, half = u, stage[2]
                        if half == 0:
                            pe.wait_ge(v_kvc.sem, v_kvc.nth(j, g + 1))
                        else:
                            pe.wait_ge(v_a.sem, v_a.nth(j, 2 * g))
                        pe.wait_ge(a_den.sem, a_den.nth(j, 2 * g + half))
                        pe.wait_ge(a_exp.sem, a_exp.nth(j, 16 * g + 8 + 4 * half + 4))
                        for bank, c in ((DN, P), (ND[half], 0)):
                            for h in range(HG):
                                last = mm(bank[DH * h:DH * (h + 1), :], KVS[:, g, c + DH * h:c + DH * (h + 1)],
                                          FE[:, h, :, 0:M], start=True, stop=True, tile_position=(0, DH * h))
                        last.then_inc(t_gg.sem, 1)
                    elif kind == "O":
                        pe.wait_ge(v_alo.sem, v_alo.nth(j, u + 1))
                        ah = ST[:, 1, D * (u % 2):D * (u % 2 + 1)]
                        al = ST[:, 1, 1024 + D * (u % 2):1024 + D * (u % 2 + 1)]
                        terms = [t for k in range(KT) for t in (
                            (ah[:, P * k:P * (k + 1)], WH["o"][:, k, :]), (ah[:, P * k:P * (k + 1)], WL["o"][:, k, :]),
                            (al[:, P * k:P * (k + 1)], WH["o"][:, k, :]))]
                        products(ps[:, :], terms).then_inc(t_o.sem, 1)
                    elif kind == "YT":
                        pe.wait_ge(a_y.sem, a_y.nth(j, u + 1))
                        for k in range(KT):
                            last = nc.tensor.transpose(ps[:, P * k:P * (k + 1)], XR[:, u % 4, P * k:P * (k + 1)], ident[:, :])
                        last.then_inc(t_yt.sem, 1)
                    elif kind == "FF":
                        pe.wait_ge(v_ylo.sem, v_ylo.nth(j, u + 1))
                        terms = [t for k in range(KT) for t in (
                            (ST[:, 1, 2048 + P * k:2048 + P * (k + 1)], WT3[:, k, :]),
                            (ST[:, 1, 2560 + P * k:2560 + P * (k + 1)], WT3[:, k, :]))]
                        products(ps[:, :], terms).then_inc(t_ff.sem, 1)

            batches(pe, program)


_INS = ["L0_attn_x", "L0_attn_Wq", "L0_attn_bq", "L0_attn_Wk", "L0_attn_bk", "L0_attn_Wv", "L0_attn_bv",
        "L0_attn_Wo", "L0_attn_bo", "L0_attn_orf", "L0_ffn_weight"]


def kernel(**inputs):
    import numpy as _np
    import concourse.bacc as _bacc
    from concourse import mybir as _mybir
    from concourse.bass_utils import run_bass_kernel_spmd as _run

    nc = _bacc.Bacc("TRN2", target_bir_lowering=False, num_devices=1)
    arrays, args = {}, []
    for name in _INS:
        a = _np.ascontiguousarray(inputs[name])
        arrays[f"in_{name}"] = a
        args.append(nc.dram_tensor(f"in_{name}", a.shape, _mybir.dt.from_np(a.dtype), kind="ExternalInput").ap())
    args.append(nc.dram_tensor("out_0", (B, L, D), _mybir.dt.float32, kind="ExternalOutput").ap())
    attention_kernel(nc, *args)
    r = _run(nc, [arrays], core_ids=[0])
    return r.results[0]["out_0"]
```
